# Optimizing a Trainium2 kernel written in Bass

```python
import numpy as np
import jax
import jax.numpy as jnp

def _softmax(x, axis=-1):
    return jax.nn.softmax(x, axis=axis)

def _gelu(x):
    return jax.nn.gelu(x, approximate=True)

def _silu(x):
    return jax.nn.silu(x)

def _sigmoid(x):
    return jax.nn.sigmoid(x)

def _layernorm(x, axis=-1, eps=1e-05):
    m = jnp.mean(x, axis=axis, keepdims=True)
    v = jnp.var(x, axis=axis, keepdims=True)
    return (x - m) / jnp.sqrt(v + eps)

def _scatter_add(tgt, idx, src, axis=0):
    return tgt.at[idx].add(src)

def _segment_sum(src, seg, n):
    return jax.ops.segment_sum(src, seg, n)
kernel_name = 'mk_early_fusion_d1_tok_img1024_r4_c33859'

def setup_inputs(seed: int=0):
    np.random.seed(seed)
    _w = jnp.asarray

    def _rec_inputs():
        import jax
        import jax.numpy as jnp
        _rk = jax.random.key(seed)
        x = 7.22013e-05 + 1.00017 * jax.random.normal(jax.random.fold_in(_rk, 1), (8, 64, 256, 4), jnp.float32)
        txt = -1.32754e-10 + 0.999995 * jax.random.normal(jax.random.fold_in(_rk, 2), (8, 128, 256), jnp.float32)
        return (x, txt)
    x, txt = _rec_inputs()

    def _L0_tok_setup():
        import jax, jax.numpy as jnp
        import numpy as np
        B, F, L, H, D = (8, 64, 256, 4, 64)
        MODEL = H * F
        WIN = 128

        def _local_mask():
            m = np.ones((L, L), dtype=bool)
            m = np.tril(m, WIN - 1)
            m = np.triu(m, -(WIN - 1))
            return jnp.asarray(m)

        def _flatten(y):
            n = y.shape[0]
            return y.transpose(0, 2, 3, 1).reshape(n, L, -1)
        key = jax.random.key(seed)
        ks = jax.random.split(key, 12)
        s = lambda n: 1.0 / np.sqrt(n)
        xav = np.sqrt(6.0 / (L + L))
        return {'x': jax.random.normal(ks[0], (B, F, L, H), jnp.float32), 'Wq_w': jax.random.normal(ks[1], (D, F), jnp.float32) * s(F), 'Wq_b': jnp.zeros((D,), jnp.float32), 'Wk_w': jax.random.normal(ks[2], (D, F), jnp.float32) * s(F), 'Wk_b': jnp.zeros((D,), jnp.float32), 'Wv_w': jax.random.normal(ks[3], (D, F), jnp.float32) * s(F), 'Wv_b': jnp.zeros((D,), jnp.float32), 'w_bias': jax.random.uniform(ks[4], (L, L), jnp.float32, -xav, xav), 'out_w': jax.random.normal(ks[5], (H * D, MODEL), jnp.float32) * s(H * D), 'out_b': jnp.zeros((MODEL,), jnp.float32), 'ln_g': jnp.ones((MODEL,), jnp.float32), 'ln_b': jnp.zeros((MODEL,), jnp.float32), 'local_mask': _local_mask()}
    _L0_tok_all = _L0_tok_setup()
    _L0_tok_in = {k: v for k, v in _L0_tok_all.items() if k in ('Wq_w', 'Wq_b', 'Wk_w', 'Wk_b', 'Wv_w', 'Wv_b', 'w_bias', 'out_w', 'out_b', 'ln_g', 'ln_b', 'local_mask')}
    del _L0_tok_all

    def _L0_attn_setup():
        import jax, jax.numpy as jnp
        import numpy as np
        B_, L_, D_MODEL = (4, 512, 256)
        EXPAND, D_STATE, D_CONV = (2, 16, 4)
        D_IN = EXPAND * D_MODEL
        DT_RANK = D_MODEL // 16
        LN_EPS = 1e-05

        def _mamba(x, W_in, conv_w, conv_b, W_x, W_dt, b_dt, A_log, D):
            Bb, L, _ = x.shape
            xz = x @ W_in
            x_in, z = (xz[..., :D_IN], xz[..., D_IN:])
            xp = jnp.pad(x_in, ((0, 0), (D_CONV - 1, 0), (0, 0)))
            xc = conv_b
            for k in range(D_CONV):
                xc = xc + xp[:, k:k + L, :] * conv_w[:, k]
            xc = jax.nn.silu(xc)
            dbc = xc @ W_x
            dt = dbc[..., :DT_RANK]
            Bm = dbc[..., DT_RANK:DT_RANK + D_STATE]
            Cm = dbc[..., DT_RANK + D_STATE:]
            delta = jax.nn.softplus(dt @ W_dt + b_dt)
            A = -jnp.exp(A_log)
            u_t = jnp.swapaxes(xc, 0, 1)
            d_t = jnp.swapaxes(delta, 0, 1)
            B_t = jnp.swapaxes(Bm, 0, 1)
            C_t = jnp.swapaxes(Cm, 0, 1)

            def step(h, inp):
                u, d, b, c = inp
                dA = jnp.exp(d[..., None] * A)
                h = h * dA + (d * u)[..., None] * b[:, None, :]
                y = jnp.einsum('bds,bs->bd', h, c)
                return (h, y)
            h0 = jnp.zeros((Bb, D_IN, D_STATE), dtype=x.dtype)
            _, ys = jax.lax.scan(step, h0, (u_t, d_t, B_t, C_t))
            y = jnp.swapaxes(ys, 0, 1) + xc * D
            y = y * jax.nn.silu(z)
            return y @ (W_in[:0, :0] if False else None) if False else y
        key = jax.random.key(seed)
        ks = jax.random.split(key, 8)
        s = 0.02
        x = jax.random.normal(ks[0], (B_, L_, D_MODEL), dtype=jnp.float32)
        W_in = jax.random.normal(ks[1], (D_MODEL, 2 * D_IN), dtype=jnp.float32) * s
        conv_w = jax.random.normal(ks[2], (D_IN, D_CONV), dtype=jnp.float32) * 0.1
        conv_b = jnp.zeros((D_IN,), dtype=jnp.float32)
        W_x = jax.random.normal(ks[3], (D_IN, DT_RANK + 2 * D_STATE), dtype=jnp.float32) * s
        W_dt = jax.random.normal(ks[4], (DT_RANK, D_IN), dtype=jnp.float32) * s
        b_dt = jnp.log(jnp.expm1(jnp.full((D_IN,), 0.01, dtype=jnp.float32)))
        A_log = jnp.log(jnp.broadcast_to(jnp.arange(1, D_STATE + 1, dtype=jnp.float32), (D_IN, D_STATE)))
        Dp = jnp.ones((D_IN,), dtype=jnp.float32)
        W_out = jax.random.normal(ks[5], (D_IN, D_MODEL), dtype=jnp.float32) * s
        gamma = jnp.ones((D_MODEL,), dtype=jnp.float32)
        beta = jnp.zeros((D_MODEL,), dtype=jnp.float32)
        return dict(x=x, W_in=W_in, conv_w=conv_w, conv_b=conv_b, W_x=W_x, W_dt=W_dt, b_dt=b_dt, A_log=A_log, D=Dp, W_out=W_out, gamma=gamma, beta=beta)
    _L0_attn_all = _L0_attn_setup()
    _L0_attn_in = {k: v for k, v in _L0_attn_all.items() if k in ('W_in', 'conv_w', 'conv_b', 'W_x', 'W_dt', 'b_dt', 'A_log', 'D', 'W_out', 'gamma', 'beta')}
    del _L0_attn_all

    def _L0_ffn_setup():
        import jax, jax.numpy as jnp
        import numpy as np
        LOOPS = 2
        NUM_GROUPS = 4
        EXPERTS_PER_GROUP = 2
        NUM_EXPERTS = NUM_GROUPS * EXPERTS_PER_GROUP
        GROUPS_TOP_K = 2
        TOP_K = 1
        RMS_EPS = 1e-06
        EPS = 1e-09

        def _rmsnorm(x, w):
            return x * jax.lax.rsqrt(jnp.mean(x * x, axis=-1, keepdims=True) + RMS_EPS) * w

        def _combine_weights(x_flat, w_macro, w_micro):
            T = x_flat.shape[0]
            macro = jax.nn.softmax(x_flat @ w_macro.T, axis=-1)
            mvals, midx = jax.lax.top_k(macro, GROUPS_TOP_K)
            mvals = mvals / (jnp.sum(mvals, axis=-1, keepdims=True) + EPS)
            micro = jax.nn.softmax(jnp.einsum('td,ged->tge', x_flat, w_micro), axis=-1)
            uvals, uidx = jax.lax.top_k(micro, TOP_K)
            uvals = uvals / (jnp.sum(uvals, axis=-1, keepdims=True) + EPS)
            tok = jnp.arange(T)
            combine = jnp.zeros((T, NUM_EXPERTS), x_flat.dtype)
            for s in range(GROUPS_TOP_K):
                g = midx[:, s]
                wg = mvals[:, s:s + 1]
                li = uidx[tok, g]
                lv = uvals[tok, g]
                eidx = g[:, None] * EXPERTS_PER_GROUP + li
                combine = combine.at[tok[:, None], eidx].add(lv * wg)
            return combine
        key = jax.random.key(seed)
        ks = jax.random.split(key, 6)
        B, S, D, F = (2, 256, 256, 512)
        return {'z': jax.random.normal(ks[0], (B, S, D), jnp.float32), 'norm_w': jnp.ones((D,), jnp.float32), 'w_macro': jax.random.normal(ks[1], (NUM_GROUPS, D), jnp.float32) * D ** (-0.5), 'w_micro': jax.random.normal(ks[2], (NUM_GROUPS, EXPERTS_PER_GROUP, D), jnp.float32) * D ** (-0.5), 'w1': jax.random.normal(ks[3], (NUM_EXPERTS, F, D), jnp.float32) * D ** (-0.5), 'w2': jax.random.normal(ks[4], (NUM_EXPERTS, D, F), jnp.float32) * F ** (-0.5)}
    _L0_ffn_all = _L0_ffn_setup()
    _L0_ffn_in = {k: v for k, v in _L0_ffn_all.items() if k in ('norm_w', 'w_macro', 'w_micro', 'w1', 'w2')}
    del _L0_ffn_all
    return {'x': x, 'txt': txt, 'L0_tok_Wq_w': _L0_tok_in['Wq_w'], 'L0_tok_Wq_b': _L0_tok_in['Wq_b'], 'L0_tok_Wk_w': _L0_tok_in['Wk_w'], 'L0_tok_Wk_b': _L0_tok_in['Wk_b'], 'L0_tok_Wv_w': _L0_tok_in['Wv_w'], 'L0_tok_Wv_b': _L0_tok_in['Wv_b'], 'L0_tok_w_bias': _L0_tok_in['w_bias'], 'L0_tok_out_w': _L0_tok_in['out_w'], 'L0_tok_out_b': _L0_tok_in['out_b'], 'L0_tok_ln_g': _L0_tok_in['ln_g'], 'L0_tok_ln_b': _L0_tok_in['ln_b'], 'L0_tok_local_mask': _L0_tok_in['local_mask'], 'L0_attn_W_in': _L0_attn_in['W_in'], 'L0_attn_conv_w': _L0_attn_in['conv_w'], 'L0_attn_conv_b': _L0_attn_in['conv_b'], 'L0_attn_W_x': _L0_attn_in['W_x'], 'L0_attn_W_dt': _L0_attn_in['W_dt'], 'L0_attn_b_dt': _L0_attn_in['b_dt'], 'L0_attn_A_log': _L0_attn_in['A_log'], 'L0_attn_D': _L0_attn_in['D'], 'L0_attn_W_out': _L0_attn_in['W_out'], 'L0_attn_gamma': _L0_attn_in['gamma'], 'L0_attn_beta': _L0_attn_in['beta'], 'L0_ffn_norm_w': _L0_ffn_in['norm_w'], 'L0_ffn_w_macro': _L0_ffn_in['w_macro'], 'L0_ffn_w_micro': _L0_ffn_in['w_micro'], 'L0_ffn_w1': _L0_ffn_in['w1'], 'L0_ffn_w2': _L0_ffn_in['w2']}

def reference(x, txt, L0_tok_Wq_w, L0_tok_Wq_b, L0_tok_Wk_w, L0_tok_Wk_b, L0_tok_Wv_w, L0_tok_Wv_b, L0_tok_w_bias, L0_tok_out_w, L0_tok_out_b, L0_tok_ln_g, L0_tok_ln_b, L0_tok_local_mask, L0_attn_W_in, L0_attn_conv_w, L0_attn_conv_b, L0_attn_W_x, L0_attn_W_dt, L0_attn_b_dt, L0_attn_A_log, L0_attn_D, L0_attn_W_out, L0_attn_gamma, L0_attn_beta, L0_ffn_norm_w, L0_ffn_w_macro, L0_ffn_w_micro, L0_ffn_w1, L0_ffn_w2):
    import jax
    import jax.numpy as jnp

    def _L0_tok_ref(x, Wq_w, Wq_b, Wk_w, Wk_b, Wv_w, Wv_b, w_bias, out_w, out_b, ln_g, ln_b, local_mask):
        import jax, jax.numpy as jnp
        import numpy as np
        B, F, L, H, D = (8, 64, 256, 4, 64)
        MODEL = H * F
        WIN = 128

        def _local_mask():
            m = np.ones((L, L), dtype=bool)
            m = np.tril(m, WIN - 1)
            m = np.triu(m, -(WIN - 1))
            return jnp.asarray(m)

        def _flatten(y):
            n = y.shape[0]
            return y.transpose(0, 2, 3, 1).reshape(n, L, -1)

        def proj(w, b):
            y = jnp.einsum('nclh,dc->ndlh', x, w) + b[None, :, None, None]
            return _flatten(y)
        q = proj(Wq_w, Wq_b)
        k = proj(Wk_w, Wk_b)
        v = proj(Wv_w, Wv_b)
        wb = w_bias * local_mask.astype(w_bias.dtype)
        ew = jnp.exp(wb)
        ek = jnp.exp(k)
        num = jnp.einsum('ts,nsd->ntd', ew, ek * v)
        den = jnp.einsum('ts,nsd->ntd', ew, ek)
        y = jax.nn.sigmoid(q) * num / den
        h = y @ out_w + out_b + _flatten(x)
        mu = jnp.mean(h, axis=-1, keepdims=True)
        var = jnp.mean(jnp.square(h - mu), axis=-1, keepdims=True)
        return (h - mu) * jax.lax.rsqrt(var + 1e-05) * ln_g + ln_b

    def _L0_attn_ref(x, W_in, conv_w, conv_b, W_x, W_dt, b_dt, A_log, D, W_out, gamma, beta):
        import jax, jax.numpy as jnp
        import numpy as np
        B_, L_, D_MODEL = (4, 512, 256)
        EXPAND, D_STATE, D_CONV = (2, 16, 4)
        D_IN = EXPAND * D_MODEL
        DT_RANK = D_MODEL // 16
        LN_EPS = 1e-05

        def _mamba(x, W_in, conv_w, conv_b, W_x, W_dt, b_dt, A_log, D):
            Bb, L, _ = x.shape
            xz = x @ W_in
            x_in, z = (xz[..., :D_IN], xz[..., D_IN:])
            xp = jnp.pad(x_in, ((0, 0), (D_CONV - 1, 0), (0, 0)))
            xc = conv_b
            for k in range(D_CONV):
                xc = xc + xp[:, k:k + L, :] * conv_w[:, k]
            xc = jax.nn.silu(xc)
            dbc = xc @ W_x
            dt = dbc[..., :DT_RANK]
            Bm = dbc[..., DT_RANK:DT_RANK + D_STATE]
            Cm = dbc[..., DT_RANK + D_STATE:]
            delta = jax.nn.softplus(dt @ W_dt + b_dt)
            A = -jnp.exp(A_log)
            u_t = jnp.swapaxes(xc, 0, 1)
            d_t = jnp.swapaxes(delta, 0, 1)
            B_t = jnp.swapaxes(Bm, 0, 1)
            C_t = jnp.swapaxes(Cm, 0, 1)

            def step(h, inp):
                u, d, b, c = inp
                dA = jnp.exp(d[..., None] * A)
                h = h * dA + (d * u)[..., None] * b[:, None, :]
                y = jnp.einsum('bds,bs->bd', h, c)
                return (h, y)
            h0 = jnp.zeros((Bb, D_IN, D_STATE), dtype=x.dtype)
            _, ys = jax.lax.scan(step, h0, (u_t, d_t, B_t, C_t))
            y = jnp.swapaxes(ys, 0, 1) + xc * D
            y = y * jax.nn.silu(z)
            return y @ (W_in[:0, :0] if False else None) if False else y
        y = _mamba(x, W_in, conv_w, conv_b, W_x, W_dt, b_dt, A_log, D) @ W_out
        h = x + y
        mu = jnp.mean(h, axis=-1, keepdims=True)
        var = jnp.mean(jnp.square(h - mu), axis=-1, keepdims=True)
        return (h - mu) / jnp.sqrt(var + LN_EPS) * gamma + beta

    def _L0_ffn_ref(z, norm_w, w_macro, w_micro, w1, w2):
        import jax, jax.numpy as jnp
        import numpy as np
        LOOPS = 2
        NUM_GROUPS = 4
        EXPERTS_PER_GROUP = 2
        NUM_EXPERTS = NUM_GROUPS * EXPERTS_PER_GROUP
        GROUPS_TOP_K = 2
        TOP_K = 1
        RMS_EPS = 1e-06
        EPS = 1e-09

        def _rmsnorm(x, w):
            return x * jax.lax.rsqrt(jnp.mean(x * x, axis=-1, keepdims=True) + RMS_EPS) * w

        def _combine_weights(x_flat, w_macro, w_micro):
            T = x_flat.shape[0]
            macro = jax.nn.softmax(x_flat @ w_macro.T, axis=-1)
            mvals, midx = jax.lax.top_k(macro, GROUPS_TOP_K)
            mvals = mvals / (jnp.sum(mvals, axis=-1, keepdims=True) + EPS)
            micro = jax.nn.softmax(jnp.einsum('td,ged->tge', x_flat, w_micro), axis=-1)
            uvals, uidx = jax.lax.top_k(micro, TOP_K)
            uvals = uvals / (jnp.sum(uvals, axis=-1, keepdims=True) + EPS)
            tok = jnp.arange(T)
            combine = jnp.zeros((T, NUM_EXPERTS), x_flat.dtype)
            for s in range(GROUPS_TOP_K):
                g = midx[:, s]
                wg = mvals[:, s:s + 1]
                li = uidx[tok, g]
                lv = uvals[tok, g]
                eidx = g[:, None] * EXPERTS_PER_GROUP + li
                combine = combine.at[tok[:, None], eidx].add(lv * wg)
            return combine
        B, S, D = z.shape
        T = B * S
        for _ in range(LOOPS):
            zn = _rmsnorm(z, norm_w)
            x = zn.reshape(T, D)
            combine = _combine_weights(x, w_macro, w_micro)
            h = jax.nn.silu(jnp.einsum('td,efd->tef', x, w1))
            y = jnp.einsum('tef,edf->ted', h, w2)
            mixed = jnp.einsum('ted,te->td', y, combine)
            z = z + mixed.reshape(B, S, D)
        return z
    h = _L0_tok_ref(x, L0_tok_Wq_w, L0_tok_Wq_b, L0_tok_Wk_w, L0_tok_Wk_b, L0_tok_Wv_w, L0_tok_Wv_b, L0_tok_w_bias, L0_tok_out_w, L0_tok_out_b, L0_tok_ln_g, L0_tok_ln_b, L0_tok_local_mask)
    h = jnp.concatenate([h, txt], axis=1)
    h = h + _L0_attn_ref(_layernorm(h, axis=-1), L0_attn_W_in, L0_attn_conv_w, L0_attn_conv_b, L0_attn_W_x, L0_attn_W_dt, L0_attn_b_dt, L0_attn_A_log, L0_attn_D, L0_attn_W_out, L0_attn_gamma, L0_attn_beta)
    h = h + _L0_ffn_ref(_layernorm(h, axis=-1), L0_ffn_norm_w, L0_ffn_w_macro, L0_ffn_w_micro, L0_ffn_w1, L0_ffn_w2)
    return h

_drawn_inputs = setup_inputs


def setup_inputs(seed=0):
    import zlib

    import numpy as np

    out = dict(_drawn_inputs(seed))
    spreads = {'L0_tok_Wq_b': (0.0, 0.667),
     'L0_tok_Wk_b': (0.0, 0.8),
     'L0_tok_Wv_b': (0.0, 0.1),
     'L0_tok_out_b': (0.0, 0.1),
     'L0_tok_ln_g': (1.0, 0.2),
     'L0_tok_ln_b': (0.0, 0.1),
     'L0_attn_conv_b': (0.0, 0.8),
     'L0_attn_b_dt': (-4.600166320800781, 0.6),
     'L0_attn_D': (1.0, 0.6),
     'L0_attn_gamma': (1.0, 0.2),
     'L0_attn_beta': (0.0, 0.1),
     'L0_ffn_norm_w': (1.0, 0.2)}
    factors = {'L0_tok_w_bias': 5.629,
     'L0_attn_W_in': 5.334,
     'L0_attn_conv_w': 7.982,
     'L0_attn_W_x': 8.0,
     'L0_attn_W_dt': 8.0,
     'L0_attn_A_log': 8.0,
     'L0_attn_W_out': 6.027}
    for name, (base, spread) in spreads.items():
        noise = np.random.default_rng([zlib.crc32(name.encode()), seed]).standard_normal(out[name].shape)
        drawn = base * np.exp(spread * noise) if base else spread * noise
        out[name] = jnp.asarray(drawn.astype(out[name].dtype))
    for name, factor in factors.items():
        out[name] = (out[name] * factor).astype(out[name].dtype)
    return out
```

```python
from contextlib import ExitStack

import concourse.bass as bass
from concourse import mybir

F32 = mybir.dt.float32
BF16 = mybir.dt.bfloat16
I32 = mybir.dt.int32
ACT = mybir.ActivationFunctionType
ALU = mybir.AluOpType
AX = mybir.AxisListType.X

P = 128
B, F, L, H = 8, 64, 256, 4
LT = 128
D = H * F
T = L + LT
TB = T // P
LB = L // P
KB = D // P
DIN = 2 * D
M = DIN // P
S = 16
R = D // 16
TAPS = 4
G, EPG = 4, 2
E = G * EPG
FF = 512
FB = FF // P
LOOPS = 2
NX = LOOPS * E
LOG = G + E
LN_EPS, RMS_EPS, TOP_EPS = 1e-5, 1e-6, 1e-9

ROWS = ("out_b", "ln_g", "ln_b", "gamma", "beta", "norm_w")
C_CONV, C_CONVB, C_BDT, C_D, C_A = 0, TAPS, TAPS + 1, TAPS + 2, TAPS + 3
CH = TAPS + 3 + S

MAMBA_HEAD = [("project", 0), ("mix", 0), ("mix_out", 0), ("widen", 0), ("states_in", 0), ("delta", 0)]


def schedule(mamba, experts):
    x_steps = []
    for loop in range(LOOPS):
        x_steps.append(("route", loop))
        x_steps += [("expert", loop * E + e) for e in range(E)]
        x_steps.append(("last_expert", loop))
    x_steps.append(("store", 0))
    m_steps = MAMBA_HEAD + [("scan", s) for s in range(S)]
    steps = [("load", 0)] if mamba else []
    if not experts:
        return steps + m_steps + [("mamba_out", 0)]
    if not mamba:
        return steps + x_steps
    while x_steps or m_steps:
        steps += x_steps[:1]
        del x_steps[:1]
        steps += m_steps[:1]
        del m_steps[:1]
    return steps + [("mamba_out", 0)]


def fusion_kernel(nc, x, txt, w_qkv, w_bias_t, mask_t, out_w, rows, w_in, chan, w_x, w_dt, w_out,
                  w_route, w1, w2, ident, pick, lower, out):
    with ExitStack() as ctx:
        def sb(name, shape, dt=F32):
            return ctx.enter_context(nc.sbuf_tensor(name, shape, dt))

        def pb(name, shape):
            return ctx.enter_context(nc.psum_tensor(name, shape, F32))

        sems = {}

        def sem(name):
            sems[name] = ctx.enter_context(nc.semaphore(name))
            return sems[name]

        W1 = sb("W1", [P, E, KB, FF])
        W2 = sb("W2", [P, E, FB, D])
        WIN = sb("WIN", [P, KB, 2 * DIN])
        WX = sb("WX", [P, M, P])
        WDT = sb("WDT", [R, DIN])
        WOUT = sb("WOUT", [P, M, D])
        OW = sb("OW", [P, KB, D])
        WQ = sb("WQ", [F + 1, 4 * F])
        EWT = sb("EWT", [P, LB, L])
        ROW = sb("ROW", [P, len(ROWS), D])
        CHAN = sb("CHAN", [P, M, CH])
        WR = sb("WR", [P, KB, LOG])
        IDENT = sb("IDENT", [P, P])
        PICKF = sb("PICKF", [P, 2 * S])
        PICK = sb("PICK", [P, 2 * S], BF16)
        LOWER = sb("LOWER", [P, TB, G * G])
        HALF = sb("HALF", [P, TB])
        X = sb("X", [F + 1, H, L])
        YTT = sb("YTT", [P, KB, L])
        H1 = sb("H1", [P, TB, D])
        X2 = sb("X2", [P, TB, D])
        X2T = sb("X2T", [P, KB, T])
        STAT = sb("STAT", [P, TB, 6])
        MV = sb("MV", [P, TB, 2])
        VE = sb("VE", [P, TB])
        RSTD = sb("RSTD", [P, TB])
        U = sb("U", [P, M, T])
        SZ = sb("SZ", [P, M, T])
        DT = sb("DT", [R, T])
        BC3 = sb("BC3", [P, T], BF16)
        HI = sb("HI", [P, T], BF16)
        REST = sb("REST", [P, T])
        DEL = sb("DEL", [P, M, T])
        DU = sb("DU", [P, M, T])
        Y = sb("Y", [P, M, T])
        DA = sb("DA", [P, 2, M, T])
        DB = sb("DB", [P, M, T])
        HS = sb("HS", [P, M, T])
        HC = sb("HC", [P, 2, M, T])
        XB, EX, CONV = DB, HS, HS
        OPE, LNO = HC[:, 0], HC[:, 1]
        scratch = HC[:, :, :, :].rearrange("p a m t -> p (a m t)")
        EK = scratch[:, 0:1024].rearrange("p (b n) -> p b n", b=LB)
        SG = scratch[:, 1024:1536].rearrange("p (b n) -> p b n", b=LB)
        RES = scratch[:, 1536:2048].rearrange("p (b n) -> p b n", b=LB)
        YT = scratch[:, 2048:2560].rearrange("p (b n) -> p b n", b=LB)
        DD = scratch[:, 2560:3072].rearrange("p (b n) -> p b n", b=LB)
        MASK = scratch[:, 0:LB * L].bitcast(I32).rearrange("p (b n) -> p b n", b=LB)
        H2 = sb("H2", [P, TB, D])
        Z = sb("Z", [P, TB, D])
        ZN = sb("ZN", [P, TB, D])
        OUT = ZN
        ZNT = sb("ZNT", [P, KB, T])
        HH = sb("HH", [P, 2, FB, T])
        SS = sb("SS", [P, TB])
        SSE = sb("SSE", [P, TB])
        RMS = sb("RMS", [P, TB])
        LG = sb("LG", [P, TB, LOG])
        PR = sb("PR", [P, TB, LOG])
        MX = sb("MX", [P, TB, 1 + G])
        SM = sb("SM", [P, TB, 1 + G])
        RK = sb("RK", [P, 2, TB, G * G])
        RANK = sb("RANK", [P, TB, G])
        TOP = sb("TOP", [P, 6, TB, G])
        TS = sb("TS", [P, 2, TB])
        COMB = sb("COMB", [P, TB, E])

        HP = pb("HP", [P, 2, 512])
        YP = pb("YP", [P, 2, 512])
        MP = pb("MP", [P, 4, 512])

        def y_out(tb):
            return YP[:, tb // 2, (tb % 2) * D:(tb % 2 + 1) * D]

        LGP = YP[:, 1, D:D + TB * LOG]

        weights_in = ctx.enter_context(nc.semaphore("weights_in"))
        mask_in = ctx.enter_context(nc.semaphore("mask_in"))
        v_prep = ctx.enter_context(nc.semaphore("v_prep"))
        prepared = ctx.enter_context(nc.semaphore("prepared"))
        prep_chain = ctx.enter_context(nc.semaphore("prep_chain"))
        arrived = ctx.enter_context(nc.semaphore("arrived"))
        go = ctx.enter_context(nc.semaphore("go"))
        sp_seen = ctx.enter_context(nc.semaphore("sp_seen"))

        x_in = sem("x_in")
        v_chain = sem("v_chain")
        s_chain = sem("s_chain")
        g_chain = sem("g_chain")
        proj_done = sem("proj_done")
        q_exped = sem("q_exped")
        k_exped = sem("k_exped")
        kv_made = sem("kv_made")
        res_made = sem("res_made")
        mixed = sem("mixed")
        yt_made = sem("yt_made")
        yt_turned = sem("yt_turned")
        ytt_copied = sem("ytt_copied")
        out_projected = sem("out_projected")
        var1, rstd1 = sem("var1"), sem("rstd1")
        var2, rstd2 = sem("var2"), sem("rstd2")
        var3, rstd3 = sem("var3"), sem("rstd3")
        var4, rstd4 = sem("var4"), sem("rstd4")
        h1_scaled = sem("h1_scaled")
        h1_made = sem("h1_made")
        x2_made = sem("x2_made")
        x2_turned = sem("x2_turned")
        x2t_copied = sem("x2t_copied")
        widened = sem("widened")
        conv_done = sem("conv_done")
        u_made = sem("u_made")
        sz_made = sem("sz_made")
        dbc_done = sem("dbc_done")
        dt_copied = sem("dt_copied")
        bc_split = sem("bc_split")
        delta_done = sem("delta_done")
        xb_made = sem("xb_made")
        ex_made = sem("ex_made")
        ope_made = sem("ope_made")
        ln_made = sem("ln_made")
        del_made = sem("del_made")
        y_started = sem("y_started")
        bc_cast = sem("bc_cast")
        da_made = sem("da_made")
        db_made = sem("db_made")
        scanned = sem("scanned")
        hc_made = sem("hc_made")
        y_summed = sem("y_summed")
        y_gated = sem("y_gated")
        mamba_projected = sem("mamba_projected")
        squares = sem("squares")
        ms_made, rms_made = sem("ms_made"), sem("rms_made")
        zn_made = sem("zn_made")
        zn_turned = sem("zn_turned")
        znt_copied = sem("znt_copied")
        logits_done = sem("logits_done")
        lg_shifted, lg_exped = sem("lg_shifted"), sem("lg_exped")
        routed = sem("routed")
        hidden = sem("hidden")
        silued = sem("silued")
        y_done = sem("y_done")
        y_added = sem("y_added")
        out_made = sem("out_made")
        stored = sem("stored")
        first, last = min(s.num for s in sems.values()), max(s.num for s in sems.values())
        assert last - first + 1 == len(sems)

        def run(eng, emit, meet):
            emit(eng, 0, True, False)
            meet(eng, 0)
            with eng.Fori(1, B) as i:
                emit(eng, i, True, True)
                meet(eng, i)
            emit(eng, B, False, True)

        def meet(eng, i):
            eng.drain().then_inc(arrived, 1)
            eng.wait_ge(go, i + 1)

        block = ctx.enter_context(nc.Block())

        @block.sync
        def _(sp):
            loads = [(WQ[:, :], w_qkv), (EWT[:, :, :], w_bias_t), (OW[:, :, :], out_w),
                     (ROW[:, :, :], rows), (IDENT[:, :], ident), (WIN[:, :, :], w_in),
                     (CHAN[:, :, :], chan), (WX[:, :, :], w_x), (WDT[:, :], w_dt), (WOUT[:, :, :], w_out),
                     (WR[:, :, :], w_route), (PICKF[:, :], pick), (LOWER[:, :, :], lower),
                     (W1[:, :, :, :], w1), (W2[:, :, :, :], w2)]
            sp.dma_start(MASK, mask_t).then_inc(mask_in, 16)
            for dst, src in loads:
                sp.dma_start(dst, src).then_inc(weights_in, 16)

            def emit(eng, i, mamba, experts):
                for stage, _k in schedule(mamba, experts):
                    if stage == "load":
                        if isinstance(i, int):
                            xi, ti = x[i], txt[i]
                        else:
                            xi = x[bass.ds(i, 1), :, :, :].rearrange("a c h l -> (a c) h l")
                            ti = txt[bass.ds(i, 1), :, :].rearrange("a t d -> (a t) d")
                        eng.dma_start(X[0:F, :, :], xi).then_inc(x_in, 16)
                        eng.dma_start(H1[:, LB, :], ti).then_inc(x_in, 16)
                    if stage == "store":
                        eng.wait_ge(out_made, 1)
                        if isinstance(i, int):
                            oi = out[i - 1].rearrange("(b p) d -> p b d", p=P)
                        else:
                            oi = out[bass.ds(i - 1, 1), :, :].rearrange("a (b p) d -> p (a b) d", p=P)
                        eng.dma_start(oi, OUT[:, :, :]).then_inc(stored, 16)
                        eng.wait_ge(stored, 16)

            def meet_sp(eng, i):
                turn = i + 1 if isinstance(i, int) else eng.snap(i + 1)
                eng.sem_inc(arrived, 1)
                eng.wait_ge(go, turn)
                eng.sem_inc(sp_seen, 1)

            run(sp, emit, meet_sp)

        @block.tensor
        def _(pe):
            pe.wait_ge(prepared, 3)

            def emit(pe, i, mamba, experts):
                def mix_matmul(out_, lhsT, rhs, k, n):
                    return nc.tensor.matmul(out_, lhsT, rhs, start=(k == 0), stop=(k == n - 1))

                def second_layer(n):
                    e = n % E
                    pe.wait_ge(silued, FB * (n + 1))
                    if n:
                        pe.wait_ge(y_added, n)
                    if n == E:
                        pe.wait_ge(lg_shifted, 2)
                    for tb in range(TB):
                        for fb in range(FB):
                            mm = mix_matmul(y_out(tb), HH[:, n % 2, fb, tb * P:(tb + 1) * P], W2[:, e, fb, :], fb, FB)
                    mm.then_inc(y_done, 1)

                for stage, k in schedule(mamba, experts):
                    if stage == "project":
                        pe.wait_ge(x_in, 32)
                        for lb in range(LB):
                            for h in range(H):
                                mm = mix_matmul(MP[:, 2 * lb + h // 2, (h % 2) * D:(h % 2 + 1) * D],
                                                X[:, h, lb * P:(lb + 1) * P], WQ[:, :], 0, 1)
                            mm.then_inc(proj_done, 1)
                    elif stage == "mix":
                        pe.wait_ge(kv_made, LB)
                        pe.wait_ge(res_made, LB)
                        pe.wait_ge(q_exped, LB)
                        for tb in range(LB):
                            for s in range(LB):
                                mm = mix_matmul(MP[:, tb, :], EWT[:, s, tb * P:(tb + 1) * P], EK[:, s, :], s, LB)
                            mm.then_inc(mixed, 1)
                    elif stage == "mix_out":
                        pe.wait_ge(yt_made, 1)
                        for kb in range(KB):
                            for tb in range(LB):
                                mm = nc.tensor.transpose(MP[:, 2, kb * L + tb * P:kb * L + (tb + 1) * P],
                                                         YT[:, tb, kb * P:(kb + 1) * P], IDENT[:, :])
                        mm.then_inc(yt_turned, 1)
                        pe.wait_ge(ytt_copied, 1)
                        for tb in range(LB):
                            for kb in range(KB):
                                mm = mix_matmul(MP[:, 3, tb * D:(tb + 1) * D], YTT[:, kb, tb * P:(tb + 1) * P],
                                                OW[:, kb, :], kb, KB)
                        mm.then_inc(out_projected, 1)
                    elif stage == "widen":
                        pe.wait_ge(x2_made, 1)
                        for kb in range(KB):
                            for tb in range(TB):
                                mm = nc.tensor.transpose(MP[:, kb, tb * P:(tb + 1) * P],
                                                         X2[:, tb, kb * P:(kb + 1) * P], IDENT[:, :])
                        mm.then_inc(x2_turned, 1)
                        pe.wait_ge(x2t_copied, 1)
                        for m in range(2 * M):
                            if m >= M:
                                pe.wait_ge(conv_done, m - M + 1)
                            for kb in range(KB):
                                mm = mix_matmul(MP[:, (m + 2) % 4, 0:T], WIN[:, kb, m * P:(m + 1) * P],
                                                X2T[:, kb, :], kb, KB)
                            mm.then_inc(widened, 1)
                    elif stage == "states_in":
                        pe.wait_ge(u_made, M)
                        pe.wait_ge(sz_made, 1)
                        for m in range(M):
                            mm = mix_matmul(MP[:, 2, 0:T], WX[:, m, :], U[:, m, :], m, M)
                        mm.then_inc(dbc_done, 1)
                    elif stage == "delta":
                        pe.wait_ge(dt_copied, 1)
                        pe.wait_ge(sz_made, M)
                        for m in range(M):
                            if m == M - 1:
                                pe.wait_ge(bc_split, 1)
                            mix_matmul(MP[:, (m + 3) % 4, 0:T], WDT[:, m * P:(m + 1) * P], DT[:, :], 0, 1)\
                                .then_inc(delta_done, 1)
                    elif stage == "scan":
                        if k == 0:
                            pe.wait_ge(xb_made, M)
                            pe.wait_ge(bc_split, 1)
                        if k >= 2:
                            pe.wait_ge(db_made, k - 1)
                        mix_matmul(MP[:, k % 2, 0:T], PICK[:, k:k + 1].to_broadcast([P, P]), BC3[:, :], 0, 1)
                        if k >= 2:
                            pe.wait_ge(hc_made, k - 1)
                        mix_matmul(MP[:, 2 + k % 2, 0:T], PICK[:, S + k:S + k + 1].to_broadcast([P, P]), BC3[:, :], 0, 1)\
                            .then_inc(bc_cast, 1)
                    elif stage == "mamba_out":
                        pe.wait_ge(y_gated, 1)
                        for tb in range(TB):
                            for m in range(M):
                                mm = mix_matmul(MP[:, tb // 2, (tb % 2) * D:(tb % 2 + 1) * D],
                                                Y[:, m, tb * P:(tb + 1) * P], WOUT[:, m, :], m, M)
                        mm.then_inc(mamba_projected, 1)
                    elif stage == "route":
                        pe.wait_ge(zn_made, k + 1)
                        if k:
                            pe.wait_ge(silued, FB * E * k)
                        for kb in range(KB):
                            for tb in range(TB):
                                mm = nc.tensor.transpose(HP[:, kb, tb * P:(tb + 1) * P],
                                                         ZN[:, tb, kb * P:(kb + 1) * P], IDENT[:, :])
                        mm.then_inc(zn_turned, 1)
                        pe.wait_ge(znt_copied, k + 1)
                        for tb in range(TB):
                            for kb in range(KB):
                                mm = mix_matmul(LGP[:, tb * LOG:(tb + 1) * LOG], ZNT[:, kb, tb * P:(tb + 1) * P],
                                                WR[:, kb, :], kb, KB)
                        mm.then_inc(logits_done, 1)
                    elif stage == "expert":
                        for fb in range(FB):
                            n = FB * k + fb
                            if n % (FB * E) >= 2:
                                pe.wait_ge(silued, n - 1)
                            for kb in range(KB):
                                mm = mix_matmul(HP[:, fb % 2, 0:T], W1[:, k % E, kb, fb * P:(fb + 1) * P],
                                                ZNT[:, kb, :], kb, KB)
                            mm.then_inc(hidden, 1)
                        if k % E:
                            second_layer(k - 1)
                    elif stage == "last_expert":
                        second_layer(E * k + E - 1)

            run(pe, emit, meet)

        @block.scalar
        def _(act):
            act.wait_ge(weights_in, 16 * 15)
            act.wait_ge(prep_chain, 1)
            nc.scalar.activation(EWT[:, :, :], EWT[:, :, :], ACT.Exp).then_inc(prepared, 1)
            nc.scalar.activation(CHAN[:, :, C_A:], CHAN[:, :, C_A:], ACT.Exp).then_inc(prep_chain, 1)
            act.wait_ge(prep_chain, 2)
            nc.scalar.mul(CHAN[:, :, C_A:], CHAN[:, :, C_A:], -1.0).then_inc(prepared, 1)
            act.wait_ge(prepared, 3)

            def emit(act, i, mamba, experts):
                for stage, k in schedule(mamba, experts):
                    if stage == "project":
                        for lb in range(LB):
                            act.wait_ge(proj_done, lb + 1)
                            pj = MP[:, 2 * lb:2 * lb + 2, :].rearrange("p b (h n) -> p (b h) n", n=D)
                            nc.scalar.activation(EK[:, lb, D:].rearrange("p (h n) -> p h n", h=H), pj[:, :, F:2 * F],
                                                 ACT.Exp).then_inc(k_exped, 1)
                            nc.scalar.activation(SG[:, lb, :].rearrange("p (h n) -> p h n", h=H), pj[:, :, 0:F],
                                                 ACT.Exp, scale=-1.0).then_inc(q_exped, 1)
                    elif stage == "mix_out":
                        act.wait_ge(yt_turned, 1)
                        nc.scalar.activation(YTT[:, :, :].rearrange("p k t -> p (k t)"), MP[:, 2, :],
                                             ACT.Copy).then_inc(ytt_copied, 1)
                    elif stage == "widen":
                        act.wait_ge(x2_turned, 1)
                        nc.scalar.activation(X2T[:, :, :], MP[:, 0:KB, 0:T], ACT.Copy).then_inc(x2t_copied, 1)
                        for m in range(M):
                            act.wait_ge(conv_done, m + 1)
                            nc.scalar.activation(U[:, m, :], CONV[:, m, :], ACT.Silu).then_inc(u_made, 1)
                        for m in range(M):
                            act.wait_ge(widened, M + m + 1)
                            nc.scalar.activation(SZ[:, m, :], MP[:, (m + 2) % 4, 0:T], ACT.Silu).then_inc(sz_made, 1)
                    elif stage == "states_in":
                        act.wait_ge(dbc_done, 1)
                        nc.scalar.activation(DT[:, :], MP[0:R, 2, 0:T], ACT.Copy).then_inc(dt_copied, 1)
                    elif stage == "delta":
                        act.wait_ge(u_made, M)
                        for m in range(M):
                            act.wait_ge(delta_done, m + 1)
                            nc.scalar.activation(XB[:, m, :], MP[:, (m + 3) % 4, 0:T], ACT.Identity,
                                                 bias=CHAN[:, m, C_BDT:C_BDT + 1]).then_inc(xb_made, 1)
                        act.wait_ge(xb_made, M)
                        nc.scalar.activation(EX[:, :, :], XB[:, :, :], ACT.Abs).then_inc(s_chain, 1)
                        act.wait_ge(s_chain, 1)
                        nc.scalar.activation(EX[:, :, :], EX[:, :, :], ACT.Exp, scale=-1.0).then_inc(ex_made, 1)
                        act.wait_ge(ope_made, 1)
                        nc.scalar.activation(LNO, OPE, ACT.Ln).then_inc(ln_made, 1)
                    elif stage == "scan":
                        if k == 0:
                            act.wait_ge(del_made, 1)
                        if k >= 2:
                            act.wait_ge(scanned, k - 1)
                        for m in range(M):
                            ins = nc.scalar.activation(DA[:, k % 2, m, 1:], DEL[:, m, 1:], ACT.Exp,
                                                       scale=CHAN[:, m, C_A + k:C_A + k + 1])
                        ins.then_inc(da_made, 1)
                    elif stage == "route":
                        if k:
                            act.wait_ge(y_added, E * k)
                        for tb in range(TB):
                            ins = nc.scalar.activation(ZN[:, tb, :], Z[:, tb, :], ACT.Square,
                                                       accum_out=SS[:, tb:tb + 1])
                            ins.then_inc(squares, 1)
                        act.wait_ge(zn_turned, k + 1)
                        nc.scalar.activation(ZNT[:, :, :], HP[:, :, 0:T], ACT.Copy).then_inc(znt_copied, 1)
                        act.wait_ge(lg_shifted, 2 * k + 2)
                        nc.scalar.activation(PR[:, :, :], LG[:, :, :], ACT.Exp).then_inc(lg_exped, 1)
                    elif stage == "expert":
                        if k >= 2:
                            act.wait_ge(y_done, k - 1)
                        for fb in range(FB):
                            act.wait_ge(hidden, FB * k + fb + 1)
                            nc.scalar.activation(HH[:, k % 2, fb, :], HP[:, fb % 2, 0:T], ACT.Silu)\
                                .then_inc(silued, 1)

            run(act, emit, meet)

        @block.vector
        def _(dve):
            v = nc.vector
            dve.wait_ge(weights_in, 16 * 15)
            dve.wait_ge(mask_in, 16)
            v.tensor_tensor(EWT[:, :, :], EWT[:, :, :], MASK, ALU.mult).then_inc(prep_chain, 1)
            v.tensor_copy(PICK[:, :], PICKF[:, :]).then_inc(v_prep, 1)
            v.memset(DA[:, :, :, 0:1], 0.0).then_inc(v_prep, 1)
            v.memset(BC3[0:32, :], 0.0).then_inc(v_prep, 1)
            v.memset(HALF[:, :], -0.5).then_inc(v_prep, 1)
            v.memset(X[F:F + 1, :, :], 1.0).then_inc(v_prep, 1)
            dve.wait_ge(v_prep, 5)
            dve.drain().then_inc(prepared, 1)
            dve.wait_ge(prepared, 3)

            def emit(dve, i, mamba, experts):
                count = [0]

                def link(ins):
                    count[0] += 1
                    ins.then_inc(v_chain, 1)
                    dve.wait_ge(v_chain, count[0])

                def variance(src, var):
                    for tb in range(TB if src is not None else 0):
                        ins = v.bn_stats(STAT[:, tb, :], src[:, tb, :])
                        if tb < TB - 1:
                            ins.then_inc(v_chain, 1)
                            count[0] += 1
                    link(ins)
                    for tb in range(TB):
                        ins = v.bn_aggr(MV[:, tb, :], STAT[:, tb, :])
                        if tb < TB - 1:
                            ins.then_inc(v_chain, 1)
                            count[0] += 1
                    link(ins)
                    v.tensor_scalar(VE[:, :], MV[:, :, 1], LN_EPS, None, ALU.add).then_inc(var, 1)

                def normalise(dst, src, blocks, rstd):
                    dve.wait_ge(rstd, 1)
                    for tb in range(blocks):
                        ins = v.tensor_scalar(dst[:, tb, :], src[:, tb, :], MV[:, tb, 0:1], RSTD[:, tb:tb + 1],
                                              ALU.subtract, ALU.mult)
                        if tb < blocks - 1:
                            ins.then_inc(v_chain, 1)
                            count[0] += 1
                    return ins

                def add_expert(n):
                    dve.wait_ge(y_done, n + 1)
                    if n:
                        dve.wait_ge(y_added, n)
                    for tb in range(TB):
                        ins = v.scalar_tensor_tensor(out=Z[:, tb, :], in0=y_out(tb), scalar=COMB[:, tb, n % E:n % E + 1],
                                                     in1=Z[:, tb, :], op0=ALU.mult, op1=ALU.add)
                        if tb < TB - 1:
                            ins.then_inc(v_chain, 1)
                            count[0] += 1
                    ins.then_inc(y_added, 1)
                    dve.wait_ge(v_chain, count[0])

                def wide(ap):
                    return ap.rearrange("p m t -> p (m t)")

                for stage, k in schedule(mamba, experts):
                    if stage == "project":
                        for lb in range(LB):
                            pj = MP[:, 2 * lb:2 * lb + 2, :].rearrange("p b (h n) -> p (b h) n", n=D)
                            dve.wait_ge(k_exped, lb + 1)
                            dve.wait_ge(q_exped, lb + 1)
                            v.tensor_tensor(EK[:, lb, 0:D].rearrange("p (h n) -> p h n", h=H),
                                            EK[:, lb, D:].rearrange("p (h n) -> p h n", h=H),
                                            pj[:, :, 2 * F:3 * F], ALU.mult).then_inc(kv_made, 1)
                            v.tensor_tensor(RES[:, lb, :].rearrange("p (h n) -> p h n", h=H),
                                            ROW[:, 0, :].rearrange("p (h n) -> p h n", h=H),
                                            pj[:, :, 3 * F:4 * F], ALU.add).then_inc(res_made, 1)
                    elif stage == "mix":
                        dve.wait_ge(q_exped, LB)
                        dve.wait_ge(mixed, LB)
                        link(v.scalar_tensor_tensor(out=DD[:, :, :], in0=SG[:, :, :], scalar=1.0,
                                                    in1=MP[:, 0:LB, D:], op0=ALU.add, op1=ALU.mult))
                        link(v.reciprocal(DD[:, :, :], DD[:, :, :]))
                        v.tensor_tensor(YT[:, :, :], DD[:, :, :], MP[:, 0:LB, 0:D], ALU.mult).then_inc(yt_made, 1)
                    elif stage == "mix_out":
                        dve.wait_ge(out_projected, 1)
                        dve.wait_ge(res_made, LB)
                        link(v.tensor_tensor(H1[:, 0:LB, :], RES[:, :, :],
                                             MP[:, 3, :].rearrange("p (b n) -> p b n", b=LB), ALU.add))
                        dve.wait_ge(x_in, 32)
                        variance(H1, var1)
                        normalise(X2, H1, LB, rstd1).then_inc(h1_scaled, 1)
                        dve.wait_ge(h1_made, 1)
                        variance(H1, var2)
                        normalise(X2, H1, TB, rstd2).then_inc(x2_made, 1)
                    elif stage == "widen":
                        for m in range(M):
                            dve.wait_ge(widened, m + 1)
                            xin = MP[:, (m + 2) % 4, 0:T]
                            link(v.tensor_scalar(CONV[:, m, :], xin, CHAN[:, m, TAPS - 1:TAPS],
                                                 CHAN[:, m, C_CONVB:C_CONVB + 1], ALU.mult, ALU.add))
                            for j in range(1, TAPS):
                                ins = v.scalar_tensor_tensor(out=CONV[:, m, j:], in0=xin[:, 0:T - j],
                                                             scalar=CHAN[:, m, TAPS - 1 - j:TAPS - j],
                                                             in1=CONV[:, m, j:], op0=ALU.mult, op1=ALU.add)
                                if j < TAPS - 1:
                                    link(ins)
                                else:
                                    ins.then_inc(conv_done, 1)
                    elif stage == "states_in":
                        dve.wait_ge(dt_copied, 1)
                        for q in (1, 2, 3):
                            a, b = 32 * q, 32 * q + 32
                            src = MP[a:b, 2, 0:T]
                            if q == 1:
                                link(v.tensor_copy(BC3[a:b, :], src))
                                continue
                            link(v.tensor_copy(HI[a:b, :], src))
                            if q == 2:
                                link(v.tensor_tensor(BC3[a:b, :], src, HI[a:b, :], ALU.subtract))
                                continue
                            link(v.tensor_tensor(REST[a:b, :], src, HI[a:b, :], ALU.subtract))
                            link(v.tensor_copy(HI[a:b, :], REST[a:b, :]))
                            v.tensor_tensor(BC3[a:b, :], REST[a:b, :], HI[a:b, :], ALU.subtract).then_inc(bc_split, 1)
                    elif stage == "delta":
                        dve.wait_ge(ex_made, 1)
                        v.tensor_scalar(OPE, EX[:, :, :], 1.0, None, ALU.add).then_inc(ope_made, 1)
                        dve.wait_ge(ope_made, 1)
                        link(v.scalar_tensor_tensor(out=wide(EX[:, :, :]), in0=wide(OPE), scalar=-1.0, in1=wide(EX[:, :, :]),
                                                    op0=ALU.add, op1=ALU.subtract))
                        dve.wait_ge(ln_made, 1)
                        link(v.tensor_tensor(EX[:, :, :], LNO, EX[:, :, :], ALU.subtract))
                        v.scalar_tensor_tensor(out=wide(DEL[:, :, :]), in0=wide(XB[:, :, :]), scalar=0.0,
                                               in1=wide(EX[:, :, :]), op0=ALU.max, op1=ALU.add).then_inc(del_made, 1)
                        dve.wait_ge(del_made, 1)
                        dve.wait_ge(u_made, M)
                        link(v.tensor_tensor(DU[:, :, :], DEL[:, :, :], U[:, :, :], ALU.mult))
                    elif stage == "scan":
                        dve.wait_ge(bc_cast, k + 1)
                        if k:
                            dve.wait_ge(scanned, k)
                        v.tensor_tensor(DB[:, :, :], DU[:, :, :],
                                        MP[:, k % 2, 0:T].unsqueeze(1).to_broadcast([P, M, T]), ALU.mult)\
                            .then_inc(db_made, 1)
                        dve.wait_ge(da_made, k + 1)
                        dve.wait_ge(db_made, k + 1)
                        if k:
                            dve.wait_ge(hc_made, k)
                        v.tensor_tensor_scan(wide(HS[:, :, :]), wide(DA[:, k % 2]), wide(DB[:, :, :]), 0.0,
                                             ALU.mult, ALU.add).then_inc(scanned, 1)
                        dve.wait_ge(scanned, k + 1)
                        if k >= 2:
                            dve.wait_ge(y_summed, k - 1)
                        v.tensor_tensor(HC[:, k % 2], HS[:, :, :],
                                        MP[:, 2 + k % 2, 0:T].unsqueeze(1).to_broadcast([P, M, T]), ALU.mult)\
                            .then_inc(hc_made, 1)
                    elif stage == "mamba_out":
                        dve.wait_ge(y_summed, S)
                        v.tensor_tensor(Y[:, :, :], Y[:, :, :], SZ[:, :, :], ALU.mult).then_inc(y_gated, 1)
                        dve.wait_ge(mamba_projected, 1)
                        link(v.tensor_tensor(X2[:, 0:2, :], X2[:, 0:2, :],
                                             MP[:, 0, :].rearrange("p (b n) -> p b n", b=2), ALU.add))
                        link(v.tensor_tensor(X2[:, 2, :], X2[:, 2, :], MP[:, 1, 0:D], ALU.add))
                        variance(X2, var3)
                        link(normalise(X2, X2, TB, rstd3))
                        link(v.tensor_tensor(X2[:, :, :], X2[:, :, :],
                                             ROW[:, 3:4, :].to_broadcast([P, TB, D]), ALU.mult))
                        link(v.tensor_tensor(X2[:, :, :], X2[:, :, :],
                                             ROW[:, 4:5, :].to_broadcast([P, TB, D]), ALU.add))
                        if experts:
                            dve.wait_ge(out_made, 1)
                        link(v.tensor_tensor(H2[:, :, :], H1[:, :, :], X2[:, :, :], ALU.add))
                        variance(H2, var4)
                        link(normalise(Z, H2, TB, rstd4))
                    elif stage == "route":
                        dve.wait_ge(squares, TB * (k + 1))
                        v.tensor_scalar(SSE[:, :], SS[:, :], 1.0 / D, RMS_EPS, ALU.mult, ALU.add).then_inc(ms_made, 1)
                        dve.wait_ge(rms_made, k + 1)
                        for tb in range(TB):
                            ins = v.scalar_tensor_tensor(out=ZN[:, tb, :], in0=Z[:, tb, :], scalar=RMS[:, tb:tb + 1],
                                                         in1=ROW[:, 5, :], op0=ALU.mult, op1=ALU.mult)
                            if tb < TB - 1:
                                ins.then_inc(v_chain, 1)
                                count[0] += 1
                        ins.then_inc(zn_made, 1)
                        dve.wait_ge(logits_done, k + 1)
                        lgp = LGP.rearrange("p (b n) -> p b n", b=TB)
                        link(v.tensor_copy(LG[:, :, :], lgp))
                        link(v.tensor_reduce(MX[:, :, 0], LG[:, :, 0:G], AX, ALU.max))
                        link(v.tensor_reduce(MX[:, :, 1:],
                                             LG[:, :, G:].rearrange("p b (g e) -> p b g e", e=EPG), AX, ALU.max))
                        v.tensor_tensor(LG[:, :, 0:G], LG[:, :, 0:G], MX[:, :, 0:1].to_broadcast([P, TB, G]),
                                        ALU.subtract).then_inc(lg_shifted, 1)
                        v.tensor_tensor(LG[:, :, G:].rearrange("p b (g e) -> p b g e", e=EPG),
                                        LG[:, :, G:].rearrange("p b (g e) -> p b g e", e=EPG),
                                        MX[:, :, 1:].unsqueeze(3).to_broadcast([P, TB, G, EPG]),
                                        ALU.subtract).then_inc(lg_shifted, 1)
                        dve.wait_ge(lg_exped, k + 1)
                        macro = PR[:, :, 0:G]
                        micro = PR[:, :, G:].rearrange("p b (g e) -> p b g e", e=EPG)
                        link(v.tensor_reduce(SM[:, :, 0], macro, AX, ALU.add))
                        link(v.tensor_reduce(SM[:, :, 1:], micro, AX, ALU.add))
                        link(v.reciprocal(SM[:, :, :], SM[:, :, :]))
                        link(v.tensor_tensor(macro, macro, SM[:, :, 0:1].to_broadcast([P, TB, G]), ALU.mult))
                        link(v.tensor_tensor(micro, micro, SM[:, :, 1:].unsqueeze(3).to_broadcast([P, TB, G, EPG]),
                                             ALU.mult))
                        gt = RK[:, 0].rearrange("p b (g j) -> p b g j", g=G)
                        eq = RK[:, 1].rearrange("p b (g j) -> p b g j", g=G)
                        mine = macro.unsqueeze(3).to_broadcast([P, TB, G, G])
                        other = macro.unsqueeze(2).to_broadcast([P, TB, G, G])
                        link(v.tensor_tensor(gt, other, mine, ALU.is_gt))
                        link(v.tensor_tensor(eq, other, mine, ALU.is_equal))
                        link(v.tensor_tensor(RK[:, 1], RK[:, 1], LOWER[:, :, :], ALU.mult))
                        link(v.tensor_tensor(RK[:, 0], RK[:, 0], RK[:, 1], ALU.add))
                        link(v.tensor_reduce(RANK[:, :, :], gt, AX, ALU.add))
                        kept, lead, share, second, weight = (TOP[:, j] for j in range(5))
                        link(v.scalar_tensor_tensor(out=kept, in0=RANK[:, :, :], scalar=1.5, in1=macro,
                                                    op0=ALU.is_lt, op1=ALU.mult))
                        link(v.tensor_reduce(TS[:, 0], kept, AX, ALU.add))
                        link(v.tensor_scalar(TS[:, 0], TS[:, 0], TOP_EPS, None, ALU.add))
                        link(v.reciprocal(TS[:, 1], TS[:, 0]))
                        link(v.tensor_tensor(kept, kept, TS[:, 1].unsqueeze(2).to_broadcast([P, TB, G]), ALU.mult))
                        link(v.tensor_tensor(lead, micro[:, :, :, 0], micro[:, :, :, 1], ALU.max))
                        link(v.tensor_scalar(share, lead, TOP_EPS, None, ALU.add))
                        link(v.reciprocal(share, share))
                        link(v.tensor_tensor(lead, lead, share, ALU.mult))
                        link(v.tensor_tensor(weight, lead, kept, ALU.mult))
                        link(v.tensor_tensor(second, micro[:, :, :, 1], micro[:, :, :, 0], ALU.is_gt))
                        comb = COMB[:, :, :].rearrange("p b (g e) -> p b g e", e=EPG)
                        link(v.tensor_tensor(comb[:, :, :, 1], second, weight, ALU.mult))
                        link(v.tensor_tensor(comb[:, :, :, 0], weight, comb[:, :, :, 1], ALU.subtract))
                    elif stage == "expert":
                        if k % E:
                            add_expert(k - 1)
                    elif stage == "last_expert":
                        add_expert(E * k + E - 1)
                        dve.wait_ge(y_added, E * (k + 1))
                    elif stage == "store":
                        v.tensor_tensor(OUT[:, :, :], H2[:, :, :], Z[:, :, :], ALU.add).then_inc(out_made, 1)

            run(dve, emit, meet)

        @block.gpsimd
        def _(pool):
            pool.wait_ge(prepared, 3)

            def emit(pool, i, mamba, experts):
                g = nc.gpsimd

                def power(dst, src, var, rstd, n):
                    pool.wait_ge(var, n)
                    g.tensor_tensor(dst, src, HALF[:, :], ALU.pow).then_inc(rstd, 1)

                for stage, k in schedule(mamba, experts):
                    if stage == "mix_out":
                        power(RSTD[:, :], VE[:, :], var1, rstd1, 1)
                        pool.wait_ge(h1_scaled, 1)
                        g.tensor_tensor(H1[:, 0:LB, :], X2[:, 0:LB, :], ROW[:, 1:2, :].to_broadcast([P, LB, D]),
                                        ALU.mult).then_inc(g_chain, 1)
                        pool.wait_ge(g_chain, 1)
                        g.tensor_tensor(H1[:, 0:LB, :], H1[:, 0:LB, :], ROW[:, 2:3, :].to_broadcast([P, LB, D]),
                                        ALU.add).then_inc(h1_made, 1)
                        power(RSTD[:, :], VE[:, :], var2, rstd2, 1)
                    elif stage == "states_in":
                        pool.wait_ge(u_made, M)
                        for m in range(M):
                            g.tensor_scalar(Y[:, m, :], U[:, m, :], CHAN[:, m, C_D:C_D + 1], None, ALU.mult)\
                                .then_inc(y_started, 1)
                        pool.wait_ge(y_started, M)
                    elif stage == "scan":
                        pool.wait_ge(hc_made, k + 1)
                        if k:
                            pool.wait_ge(y_summed, k)
                        g.tensor_tensor(Y[:, :, :], Y[:, :, :], HC[:, k % 2], ALU.add).then_inc(y_summed, 1)
                    elif stage == "mamba_out":
                        power(RSTD[:, :], VE[:, :], var3, rstd3, 1)
                        power(RSTD[:, :], VE[:, :], var4, rstd4, 1)
                    elif stage == "route":
                        power(RMS[:, :], SSE[:, :], ms_made, rms_made, k + 1)

            def meet_pool(pool, i):
                pool.wait_ge(arrived, 4)
                pool.drain()
                pool.sem_clear(range(first, last + 1))
                pool.sem_clear(arrived)
                pool.sem_inc(go, 1)

            run(pool, emit, meet_pool)


def _blocks(a, p=P):
    import numpy as np
    return np.ascontiguousarray(np.moveaxis(a.reshape(-1, p, *a.shape[1:]), 0, 1))


def kernel(**inputs):
    import numpy as np
    import concourse.bacc as bacc
    from concourse.bass_utils import run_bass_kernel_spmd as run

    a = {k: np.asarray(v) for k, v in inputs.items()}
    t = {k.replace("L0_", ""): v for k, v in a.items()}
    eye = np.eye(F, dtype=np.float32)
    w_qkv = np.zeros((F + 1, 4 * F), np.float32)
    for j, n in enumerate("qkv"):
        w_qkv[:F, j * F:(j + 1) * F] = t[f"tok_W{n}_w"].T
        w_qkv[F, j * F:(j + 1) * F] = t[f"tok_W{n}_b"]
    w_qkv[:F, 3 * F:] = eye
    rows = np.stack([t["tok_out_b"], t["tok_ln_g"], t["tok_ln_b"], t["attn_gamma"], t["attn_beta"], t["ffn_norm_w"]])
    chan = np.concatenate([t["attn_conv_w"], t["attn_conv_b"][:, None], t["attn_b_dt"][:, None],
                           t["attn_D"][:, None], t["attn_A_log"]], axis=1)
    wx = t["attn_W_x"]
    w_x = np.zeros((DIN, P), np.float32)
    w_x[:, :R] = wx[:, :R]
    for q in (1, 2, 3):
        w_x[:, 32 * q:32 * q + 32] = wx[:, R:]
    w_route = np.concatenate([t["ffn_w_macro"], t["ffn_w_micro"].reshape(E, D)], axis=0).T
    pick = np.zeros((P, 2 * S), np.float32)
    for q in (1, 2, 3):
        pick[32 * q + np.arange(32), np.arange(32)] = 1.0
    lower = np.tril(np.ones((G, G), np.float32), -1).reshape(1, 1, G * G)
    mask_words = np.zeros((P, LB, L, 4), np.uint8)
    mask_words[..., 0] = _blocks(t["tok_local_mask"].T)
    arrays = {
        "x": a["x"].transpose(0, 1, 3, 2),
        "txt": a["txt"],
        "w_qkv": w_qkv,
        "w_bias_t": _blocks(t["tok_w_bias"].T),
        "mask_t": mask_words.view(np.int32)[..., 0],
        "out_w": _blocks(t["tok_out_w"]),
        "rows": np.broadcast_to(rows, (P, *rows.shape)),
        "w_in": _blocks(t["attn_W_in"]),
        "chan": _blocks(chan),
        "w_x": _blocks(w_x),
        "w_dt": t["attn_W_dt"],
        "w_out": _blocks(t["attn_W_out"]),
        "w_route": _blocks(np.ascontiguousarray(w_route)),
        "w1": t["ffn_w1"].reshape(E, FF, KB, P).transpose(3, 0, 2, 1),
        "w2": t["ffn_w2"].reshape(E, D, FB, P).transpose(3, 0, 2, 1),
        "ident": np.eye(P, dtype=np.float32),
        "pick": pick,
        "lower": np.broadcast_to(lower, (P, TB, G * G)),
    }
    arrays = {k: np.ascontiguousarray(v) for k, v in arrays.items()}
    nc = bacc.Bacc("TRN2", target_bir_lowering=False, num_devices=1)
    args = [nc.dram_tensor(f"in_{k}", v.shape, mybir.dt.from_np(v.dtype), kind="ExternalInput").ap()
            for k, v in arrays.items()]
    args.append(nc.dram_tensor("out_h", (B, T, D), F32, kind="ExternalOutput").ap())
    fusion_kernel(nc, *args)
    r = run(nc, [{f"in_{k}": v for k, v in arrays.items()}], core_ids=[0])
    return r.results[0]["out_h"]
```

```python
from contextlib import ExitStack

import concourse.bass as bass
from concourse import mybir

F32 = mybir.dt.float32
BF16 = mybir.dt.bfloat16
F16 = mybir.dt.float16
I32 = mybir.dt.int32
ACT = mybir.ActivationFunctionType
ALU = mybir.AluOpType
AX = mybir.AxisListType.X

P = 128
B, F, L, H = 8, 64, 256, 4
LT = 128
D = H * F
T = L + LT
TB = T // P
LB = L // P
KB = D // P
DIN = 2 * D
M = DIN // P
S = 16
R = D // 16
TAPS = 4
G, EPG = 4, 2
E = G * EPG
FF = 512
FB = FF // P
LOOPS = 2
NX = LOOPS * E
LOG = G + E
W_TOP = 2.0 ** 14
LN_EPS, RMS_EPS, TOP_EPS = 1e-5, 1e-6, 1e-9

ROWS = ("out_b", "ln_g", "ln_b", "gamma", "beta")
C_CONV, C_CONVB, C_BDT, C_D, C_A = 0, TAPS, TAPS + 1, TAPS + 2, TAPS + 3
CH = TAPS + 3 + S

BESIDE = [
    (0, "project", 0), (0, "project", 1), (1, "mix", 0), (3, "turn_mixed", 0), (4, "mix_out", 0),
    (9, "turn_x2", 0), (10, "widen_x", 0), (10, "widen_x", 1), (10, "widen_x", 2), (10, "widen_x", 3),
    (10, "u", 0), (10, "u", 1), (11, "u", 2), (12, "u", 3), (13, "states_in", 0), (14, "delta", 0),
    (15, "widen_z", 0), (15, "ln", 0),
]
for pair in range(S // 2):
    BESIDE += [(19 + 4 * pair, "decay", 2 * pair), (19 + 4 * pair, "scan", 2 * pair), (21 + 4 * pair, "scan", 2 * pair + 1)]
BESIDE += [(54, "mamba_out", 0), (60, "square", 0), (60, "route", 0), (60, "low", 0), (61, "logits", 0), (61, "weigh", 0)]
BETWEEN = 5


def schedule(mamba, experts):
    beside = [(at, name, k) for at, name, k in BESIDE if mamba]
    steps = [("load", 0)] if mamba else []

    def piece(name):
        return [(name, BETWEEN)] if mamba else []

    if not experts:
        order = [(name, k) for _, name, k in beside]
        at = order.index(("mix", 0))
        for e in range(E):
            order.insert(at, ("w1_max", e))
            at += 1 + e % 2
        order.insert(order.index(("turn_x2", 0)), ("w1_scale", 0))
        at = order.index(("turn_x2", 0)) + 1
        for e in range(E):
            order.insert(at, ("w1_split", e))
            at += 2
        steps += order
    else:
        units = []
        for n in range(1, NX + 1):
            ups = [("up", n, 0), ("up", n, 1)] if n < NX else []
            downs = [("down", n - 1, 0), ("down", n - 1, 1)]
            if n == E:
                units += downs + piece("scan_in") + [("square", 1), ("route", 1)] + piece("scan_run")
                units += [("low", 1)] + piece("scan_out") + ups[:1] + [("logits", 1)] + ups[1:] + [("weigh", 1)]
            else:
                for j in range(2):
                    units += ups[j:j + 1] + downs[j:j + 1]
        units.append(("store", 0))
        done = 0
        for unit in units:
            while beside and beside[0][0] <= done:
                steps.append(beside.pop(0)[1:])
            steps.append(unit)
            done += unit[0] in ("up", "down")
        steps += [one[1:] for one in beside]
    steps = [one if len(one) == 2 else (one[0], one[1:]) for one in steps]
    if mamba:
        steps += [("up", (NX, 0)), ("up", (NX, 1)), ("handover", 0)]
    placed = []
    for name, k in steps:
        placed.append((name, k))
        if name == "scan":
            if k != BETWEEN or not experts:
                placed += [("scan_in", k), ("scan_run", k), ("scan_out", k)]
            if k:
                placed.append(("sum_y", k - 1))
    return placed


def fusion_kernel(nc, x, txt, w_qkv, w_bias_t, mask_t, out_w, rows, w_in, chan, w_x, w_dt, w_out,
                  w_route, norm_w, w1, w2, ident, pick, lower, out):
    with ExitStack() as ctx:
        def sb(name, shape, dt=F32):
            return ctx.enter_context(nc.sbuf_tensor(name, shape, dt))

        def pb(name, shape):
            return ctx.enter_context(nc.psum_tensor(name, shape, F32))

        sems = {}

        def sem(name):
            sems[name] = ctx.enter_context(nc.semaphore(name))
            return sems[name]

        W1 = sb("W1", [P, 2, E, KB, FF], F16)
        W2 = sb("W2", [P, E, FB, D])
        WIN = sb("WIN", [P, KB, 2 * DIN])
        WX = sb("WX", [P, M, P])
        WDT = sb("WDT", [R, DIN])
        WOUT = sb("WOUT", [P, M, D])
        OW = sb("OW", [P, KB, D])
        WQ = sb("WQ", [F + 1, 4 * F])
        EWT = sb("EWT", [P, LB, L])
        ROW = sb("ROW", [P, len(ROWS), D])
        CHAN = sb("CHAN", [P, M, CH])
        WRF = sb("WRF", [P, KB, LOG])
        WR = sb("WR", [P, 2, KB, LOG], F16)
        NW = sb("NW", [P, KB])
        WMAX = sb("WMAX", [P, E + 1, KB])
        TOPW = sb("TOPW", [P, 4])
        WSCALE = sb("WSCALE", [P, KB])
        UNSCALE = sb("UNSCALE", [P, 1])
        IDENT = sb("IDENT", [P, P])
        PICKF = sb("PICKF", [P, 2 * S])
        PICK = sb("PICK", [P, 2 * S], BF16)
        LOWER = sb("LOWER", [P, TB, G * G])
        HALF = sb("HALF", [P, TB])
        X = sb("X", [F + 1, H, L])
        YTT = sb("YTT", [P, KB, L])
        H1 = sb("H1", [P, TB, D])
        X2 = sb("X2", [P, TB, D])
        X2T = sb("X2T", [P, KB, T])
        STAT = sb("STAT", [P, TB, 6])
        MV = sb("MV", [P, TB, 2])
        VE = sb("VE", [P, TB])
        RSTD = sb("RSTD", [P, TB])
        U = sb("U", [P, M, T])
        SZ = sb("SZ", [P, M, T])
        DT = sb("DT", [R, T])
        BC3 = sb("BC3", [P, T], BF16)
        DEL = sb("DEL", [P, M, T])
        DU = sb("DU", [P, M, T])
        Y = sb("Y", [P, M, T])
        DA = sb("DA", [P, 2, M, T])
        DB = sb("DB", [P, M, T])
        HS = sb("HS", [P, M, T])
        HC = sb("HC", [P, 2, M, T])
        XB, EX, CONV = DB, HS, HS
        OPE, LNO = HC[:, 0], HC[:, 1]
        scratch = HC[:, :, :, :].rearrange("p a m t -> p (a m t)")
        EK = scratch[:, 0:1024].rearrange("p (b n) -> p b n", b=LB)
        SG = scratch[:, 1024:1536].rearrange("p (b n) -> p b n", b=LB)
        RES = scratch[:, 1536:2048].rearrange("p (b n) -> p b n", b=LB)
        YT = scratch[:, 2048:2560].rearrange("p (b n) -> p b n", b=LB)
        DD = scratch[:, 2560:3072].rearrange("p (b n) -> p b n", b=LB)
        REST = scratch[:, 2048:2048 + T]
        HI = scratch[:, 2560:2560 + T // 2].bitcast(BF16)
        MASK = scratch[:, 0:LB * L].bitcast(I32).rearrange("p (b n) -> p b n", b=LB)
        H2 = sb("H2", [P, TB, D])
        Z = sb("Z", [P, TB, D])
        ZN = sb("ZN", [P, TB, D])
        OUT = scratch[:, 0:TB * D].rearrange("p (b n) -> p b n", b=TB)
        ZNT = sb("ZNT", [P, LOOPS, 2, KB, T], F16)
        HH = sb("HH", [P, 2, FB, T])
        STAGE = HH[:, :, :, :].rearrange("p a f t -> p (a f t)").rearrange("p (s k n) -> p s k n", s=3, k=KB)
        SS = sb("SS", [P, TB])
        SSE = sb("SSE", [P, TB])
        RMS = sb("RMS", [P, TB])
        LG = sb("LG", [P, TB, LOG])
        PR = sb("PR", [P, TB, LOG])
        MX = sb("MX", [P, TB, 1 + G])
        SM = sb("SM", [P, TB, 1 + G])
        RK = sb("RK", [P, 2, TB, G * G])
        RANK = sb("RANK", [P, TB, G])
        TOP = sb("TOP", [P, 6, TB, G])
        TS = sb("TS", [P, 2, TB])
        YS = sb("YS", [P, TB, D])
        COMB = sb("COMB", [P, LOOPS, TB, E])

        HP = pb("HP", [P, 2, 512])
        YP = pb("YP", [P, 2, 512])
        MP = pb("MP", [P, 4, 512])

        def y_out(tb):
            return YP[:, tb // 2, (tb % 2) * D:(tb % 2 + 1) * D]

        BANKS = (3, 0, 1, 3)
        ZTP = (MP[:, 2:4], HP)
        LGP = (MP[:, 1, D:D + TB * LOG], YP[:, 1, D:D + TB * LOG])

        weights_in = ctx.enter_context(nc.semaphore("weights_in"))
        first_x_in = ctx.enter_context(nc.semaphore("first_x_in"))
        w2_in = ctx.enter_context(nc.semaphore("w2_in"))
        mask_in = ctx.enter_context(nc.semaphore("mask_in"))
        v_prep = ctx.enter_context(nc.semaphore("v_prep"))
        prepared = ctx.enter_context(nc.semaphore("prepared"))
        prep_chain = ctx.enter_context(nc.semaphore("prep_chain"))
        arrived = ctx.enter_context(nc.semaphore("arrived"))
        go = ctx.enter_context(nc.semaphore("go"))
        sp_seen = ctx.enter_context(nc.semaphore("sp_seen"))

        x_in = sem("x_in")
        txt_in = sem("txt_in")
        v_chain = sem("v_chain")
        s_chain = sem("s_chain")
        g_chain = sem("g_chain")
        proj_done = sem("proj_done")
        q_exped = sem("q_exped")
        k_exped = sem("k_exped")
        kv_made = sem("kv_made")
        res_made = sem("res_made")
        mixed = sem("mixed")
        yt_made = sem("yt_made")
        yt_turned = sem("yt_turned")
        ytt_copied = sem("ytt_copied")
        out_projected = sem("out_projected")
        var1, rstd1 = sem("var1"), sem("rstd1")
        var2, rstd2 = sem("var2"), sem("rstd2")
        var3, rstd3 = sem("var3"), sem("rstd3")
        var4, rstd4 = sem("var4"), sem("rstd4")
        h1_scaled = sem("h1_scaled")
        h1_made = sem("h1_made")
        x2_made = sem("x2_made")
        x2_turned = sem("x2_turned")
        x2t_copied = sem("x2t_copied")
        widened = sem("widened")
        z_widened = sem("z_widened")
        conv_done = sem("conv_done")
        u_made = sem("u_made")
        sz_made = sem("sz_made")
        dbc_done = sem("dbc_done")
        dt_copied = sem("dt_copied")
        bc_split = sem("bc_split")
        delta_done = sem("delta_done")
        xb_made = sem("xb_made")
        ex_made = sem("ex_made")
        ope_made = sem("ope_made")
        ln_made = sem("ln_made")
        del_made = sem("del_made")
        y_started = sem("y_started")
        bc_cast = sem("bc_cast")
        da_made = sem("da_made")
        db_made = sem("db_made")
        scanned = sem("scanned")
        hc_made = sem("hc_made")
        y_summed = sem("y_summed")
        y_gated = sem("y_gated")
        mamba_projected = sem("mamba_projected")
        h2_copied = sem("h2_copied")
        ms_made = [sem(f"ms_made{j}") for j in range(LOOPS)]
        rms_made = [sem(f"rms_made{j}") for j in range(LOOPS)]
        zn_made = [sem(f"zn_made{j}") for j in range(LOOPS)]
        zn_turned = [sem(f"zn_turned{j}") for j in range(LOOPS)]
        znt_high = [sem(f"znt_high{j}") for j in range(LOOPS)]
        znt_low = [sem(f"znt_low{j}") for j in range(LOOPS)]
        logits_done = [sem(f"logits_done{j}") for j in range(LOOPS)]
        lg_shifted = [sem(f"lg_shifted{j}") for j in range(LOOPS)]
        lg_exped = [sem(f"lg_exped{j}") for j in range(LOOPS)]
        weighed = [sem(f"weighed{j}") for j in range(LOOPS)]
        squares = sem("squares")
        z_made = sem("z_made")
        w1_in = [sem(f"w1_in{j}") for j in range(3)]
        w1_maxed = sem("w1_maxed")
        top_in, top_out = sem("top_in"), sem("top_out")
        w1_scaled = sem("w1_scaled")
        w1_high, w1_low = sem("w1_high"), sem("w1_low")
        hidden = sem("hidden")
        silued = sem("silued")
        y_done = sem("y_done")
        y_scaled = sem("y_scaled")
        y_added = sem("y_added")
        out_made = sem("out_made")
        stored = sem("stored")
        first, last = min(s.num for s in sems.values()), max(s.num for s in sems.values())
        assert last - first + 1 == len(sems)

        def run(eng, emit, meet):
            emit(eng, 0, True, False)
            meet(eng, 0)
            with eng.Fori(1, B) as i:
                emit(eng, i, True, True)
                meet(eng, i)
            emit(eng, B, False, True)

        def meet(eng, i):
            eng.drain().then_inc(arrived, 1)
            eng.wait_ge(go, i + 1)

        block = ctx.enter_context(nc.Block())

        @block.sync
        def _(sp):
            loads = [(WQ[:, :], w_qkv), (EWT[:, :, :], w_bias_t), (OW[:, :, :], out_w),
                     (ROW[:, :, :], rows), (IDENT[:, :], ident), (WIN[:, :, :], w_in),
                     (CHAN[:, :, :], chan), (WX[:, :, :], w_x), (WDT[:, :], w_dt), (WOUT[:, :, :], w_out),
                     (WRF[:, :, :], w_route), (NW[:, :], norm_w), (PICKF[:, :], pick), (LOWER[:, :, :], lower),
                     ]
            sp.dma_start(MASK, mask_t).then_inc(mask_in, 16)
            sp.dma_start(X[0:F, :, :], x[0]).then_inc(first_x_in, 16)
            for dst, src in loads:
                sp.dma_start(dst, src).then_inc(weights_in, 16)

            def emit(eng, i, mamba, experts):
                for stage, _k in schedule(mamba, experts):
                    if stage == "load":
                        ti = txt[i] if isinstance(i, int) else txt[bass.ds(i, 1), :, :].rearrange("a t d -> (a t) d")
                        eng.dma_start(H1[:, LB, :], ti).then_inc(txt_in, 16)
                    if stage == "turn_mixed":
                        eng.wait_ge(proj_done, LB)
                        xi = x[i + 1] if isinstance(i, int) else \
                            x[bass.ds(i + 1, 1), :, :, :].rearrange("a c h l -> (a c) h l")
                        eng.dma_start(X[0:F, :, :], xi).then_inc(x_in, 16)
                    if stage in ("w1_max", "w1_split"):
                        n = _k + (E if stage == "w1_split" else 0)
                        if 3 <= n < E + 3:
                            eng.wait_ge(w1_maxed, n - 2)
                        if n >= E + 3:
                            eng.wait_ge(w1_low, KB * (n - E - 2))
                        eng.dma_start(STAGE[:, n % 3], w1[:, _k]).then_inc(w1_in[n % 3], 16)
                    if stage == "mamba_out" and not experts:
                        eng.dma_start(W2[:, :, :, :], w2).then_inc(w2_in, 16)
                        eng.wait_ge(w2_in, 16)
                    if stage == "handover":
                        eng.wait_ge(x_in, 16)
                    if stage == "store":
                        eng.wait_ge(out_made, 1)
                        if isinstance(i, int):
                            oi = out[i - 1].rearrange("(b p) d -> p b d", p=P)
                        else:
                            oi = out[bass.ds(i - 1, 1), :, :].rearrange("a (b p) d -> p (a b) d", p=P)
                        eng.dma_start(oi, OUT[:, :, :]).then_inc(stored, 16)
                        eng.wait_ge(stored, 16)

            def meet_sp(eng, i):
                turn = i + 1 if isinstance(i, int) else eng.snap(i + 1)
                eng.sem_inc(arrived, 1)
                eng.wait_ge(go, turn)
                eng.sem_inc(sp_seen, 1)

            run(sp, emit, meet_sp)

        @block.tensor
        def _(pe):
            pe.wait_ge(prepared, 3)
            pe.wait_ge(first_x_in, 16)

            def emit(pe, i, mamba, experts):
                ahead = 1 if experts else NX

                def mix_matmul(out_, lhsT, rhs, k, n):
                    return nc.tensor.matmul(out_, lhsT, rhs, start=(k == 0), stop=(k == n - 1))

                def second_layer(n, half):
                    if n:
                        pe.wait_ge(silued, FB * (n + 1 - ahead))
                    if n % E:
                        pe.wait_ge(y_scaled, TB * (n - 1 - n // E) + min(2 * half + 2, TB))
                    if n == E:
                        pe.wait_ge(y_added, TB * n)
                        if half:
                            pe.wait_ge(lg_shifted[1], 2)
                    for tb in range(2 * half, min(2 * half + 2, TB)):
                        for fb in range(FB):
                            mm = mix_matmul(y_out(tb), HH[:, n % 2, fb, tb * P:(tb + 1) * P], W2[:, n % E, fb, :], fb, FB)
                    mm.then_inc(y_done, 1)

                for stage, k in schedule(mamba, experts):
                    if stage == "project":
                        for h in range(H):
                            mm = mix_matmul(MP[:, 2 * k + h // 2, (h % 2) * D:(h % 2 + 1) * D],
                                            X[:, h, k * P:(k + 1) * P], WQ[:, :], 0, 1)
                        mm.then_inc(proj_done, 1)
                    elif stage == "mix":
                        pe.wait_ge(kv_made, LB)
                        pe.wait_ge(res_made, LB)
                        pe.wait_ge(q_exped, LB)
                        for tb in range(LB):
                            for s in range(LB):
                                mm = mix_matmul(MP[:, tb, :], EWT[:, s, tb * P:(tb + 1) * P], EK[:, s, :], s, LB)
                            mm.then_inc(mixed, 1)
                    elif stage == "turn_mixed":
                        pe.wait_ge(yt_made, 1)
                        for kb in range(KB):
                            for tb in range(LB):
                                mm = nc.tensor.transpose(MP[:, 2, kb * L + tb * P:kb * L + (tb + 1) * P],
                                                         YT[:, tb, kb * P:(kb + 1) * P], IDENT[:, :])
                        mm.then_inc(yt_turned, 1)
                    elif stage == "mix_out":
                        pe.wait_ge(ytt_copied, 1)
                        for tb in range(LB):
                            for kb in range(KB):
                                mm = mix_matmul(MP[:, 3, tb * D:(tb + 1) * D], YTT[:, kb, tb * P:(tb + 1) * P],
                                                OW[:, kb, :], kb, KB)
                        mm.then_inc(out_projected, 1)
                    elif stage == "turn_x2":
                        pe.wait_ge(x2_made, 1)
                        for kb in range(KB):
                            for tb in range(TB):
                                mm = nc.tensor.transpose(MP[:, kb, tb * P:(tb + 1) * P],
                                                         X2[:, tb, kb * P:(kb + 1) * P], IDENT[:, :])
                        mm.then_inc(x2_turned, 1)
                    elif stage == "widen_x":
                        pe.wait_ge(x2t_copied, 1)
                        for kb in range(KB):
                            mm = mix_matmul(MP[:, (k + 2) % 4, 0:T], WIN[:, kb, k * P:(k + 1) * P], X2T[:, kb, :], kb, KB)
                        mm.then_inc(widened, 1)
                    elif stage == "states_in":
                        pe.wait_ge(u_made, M)
                        for m in range(M):
                            mm = mix_matmul(MP[:, 2, 0:T], WX[:, m, :], U[:, m, :], m, M)
                        mm.then_inc(dbc_done, 1)
                    elif stage == "delta":
                        pe.wait_ge(dt_copied, 1)
                        for m in range(M):
                            if m == M - 1:
                                pe.wait_ge(xb_made, 1)
                            mix_matmul(MP[:, BANKS[m], 0:T], WDT[:, m * P:(m + 1) * P], DT[:, :], 0, 1)\
                                .then_inc(delta_done, 1)
                    elif stage == "widen_z":
                        for m in range(M):
                            if m < M - 1:
                                pe.wait_ge(xb_made, M if m == 0 else m + 1)
                            else:
                                pe.wait_ge(sz_made, 1)
                            for kb in range(KB):
                                mm = mix_matmul(MP[:, BANKS[m], 0:T], WIN[:, kb, (M + m) * P:(M + m + 1) * P],
                                                X2T[:, kb, :], kb, KB)
                            mm.then_inc(z_widened, 1)
                    elif stage == "scan":
                        if k == 0:
                            pe.wait_ge(sz_made, M)
                            pe.wait_ge(bc_split, 1)
                        if k >= 2:
                            pe.wait_ge(db_made, k - 1)
                        mix_matmul(MP[:, k % 2, 0:T], PICK[:, k:k + 1].to_broadcast([P, P]), BC3[:, :], 0, 1)
                        if k >= 2:
                            pe.wait_ge(hc_made, k - 1)
                        mix_matmul(MP[:, 2 + k % 2, 0:T], PICK[:, S + k:S + k + 1].to_broadcast([P, P]), BC3[:, :], 0, 1)\
                            .then_inc(bc_cast, 1)
                    elif stage == "mamba_out":
                        pe.wait_ge(y_gated, 1)
                        for tb in range(TB):
                            for m in range(M):
                                mm = mix_matmul(MP[:, tb // 2, (tb % 2) * D:(tb % 2 + 1) * D],
                                                Y[:, m, tb * P:(tb + 1) * P], WOUT[:, m, :], m, M)
                        mm.then_inc(mamba_projected, 1)
                    elif stage == "route":
                        if k:
                            pe.wait_ge(silued, FB * (E - ahead))
                        for tb in range(TB):
                            pe.wait_ge(zn_made[k], tb + 1)
                            for kb in range(KB):
                                mm = nc.tensor.transpose(ZTP[k][:, kb, tb * P:(tb + 1) * P],
                                                         ZN[:, tb, kb * P:(kb + 1) * P], IDENT[:, :])
                        mm.then_inc(zn_turned[k], 1)
                    elif stage == "logits":
                        pe.wait_ge(znt_low[k], 1)
                        for tb in range(TB):
                            for kb in range(KB):
                                for j, (a, b) in enumerate(((0, 0), (0, 1), (1, 0))):
                                    mm = mix_matmul(LGP[k][:, tb * LOG:(tb + 1) * LOG],
                                                    ZNT[:, k, a, kb, tb * P:(tb + 1) * P],
                                                    WR[:, b, kb, :], 3 * kb + j, 3 * KB)
                        mm.then_inc(logits_done[k], 1)
                    elif stage == "up":
                        n, half = k
                        if half == 0 and n % E == 0:
                            pe.wait_ge(znt_low[n // E % LOOPS], 1)
                        for fb in (2 * half, 2 * half + 1):
                            before = FB * (n - ahead) + fb - 2
                            if before >= 0 and (n % E or half):
                                pe.wait_ge(silued, before + 1)
                            for kb in range(KB):
                                for j, (a, b) in enumerate(((0, 0), (0, 1), (1, 0))):
                                    mm = mix_matmul(HP[:, fb % 2, 0:T], W1[:, a, n % E, kb, fb * P:(fb + 1) * P],
                                                    ZNT[:, n // E % LOOPS, b, kb, :], 3 * kb + j, 3 * KB)
                            mm.then_inc(hidden, 1)
                    elif stage == "down":
                        second_layer(*k)

            run(pe, emit, meet)

        @block.scalar
        def _(act):
            act.wait_ge(weights_in, 16 * 14)
            act.wait_ge(prep_chain, 1)
            nc.scalar.activation(EWT[:, :, :], EWT[:, :, :], ACT.Exp).then_inc(prepared, 1)
            nc.scalar.activation(CHAN[:, :, C_A:], CHAN[:, :, C_A:], ACT.Exp).then_inc(prep_chain, 1)
            act.wait_ge(prep_chain, 2)
            nc.scalar.mul(CHAN[:, :, C_A:], CHAN[:, :, C_A:], -1.0).then_inc(prepared, 1)
            act.wait_ge(prepared, 3)

            def emit(act, i, mamba, experts):
                ahead = 1 if experts else NX
                for stage, k in schedule(mamba, experts):
                    if stage == "project":
                        act.wait_ge(proj_done, k + 1)
                        pj = MP[:, 2 * k:2 * k + 2, :].rearrange("p b (h n) -> p (b h) n", n=D)
                        nc.scalar.activation(EK[:, k, D:].rearrange("p (h n) -> p h n", h=H), pj[:, :, F:2 * F],
                                             ACT.Exp).then_inc(k_exped, 1)
                        nc.scalar.activation(SG[:, k, :].rearrange("p (h n) -> p h n", h=H), pj[:, :, 0:F],
                                             ACT.Exp, scale=-1.0).then_inc(q_exped, 1)
                    elif stage == "turn_mixed":
                        act.wait_ge(yt_turned, 1)
                        nc.scalar.activation(YTT[:, :, :].rearrange("p k t -> p (k t)"), MP[:, 2, :],
                                             ACT.Copy).then_inc(ytt_copied, 1)
                    elif stage == "turn_x2":
                        act.wait_ge(x2_turned, 1)
                        nc.scalar.activation(X2T[:, :, :], MP[:, 0:KB, 0:T], ACT.Copy).then_inc(x2t_copied, 1)
                    elif stage == "u":
                        act.wait_ge(conv_done, k + 1)
                        nc.scalar.activation(U[:, k, :], CONV[:, k, :], ACT.Silu).then_inc(u_made, 1)
                    elif stage == "widen_z":
                        for m in range(M):
                            act.wait_ge(z_widened, m + 1)
                            nc.scalar.activation(SZ[:, m, :], MP[:, BANKS[m], 0:T], ACT.Silu).then_inc(sz_made, 1)
                    elif stage == "states_in":
                        act.wait_ge(dbc_done, 1)
                        nc.scalar.activation(DT[:, :], MP[0:R, 2, 0:T], ACT.Copy).then_inc(dt_copied, 1)
                    elif stage == "delta":
                        act.wait_ge(u_made, M)
                        for m in range(M):
                            act.wait_ge(delta_done, m + 1)
                            nc.scalar.activation(XB[:, m, :], MP[:, BANKS[m], 0:T], ACT.Identity,
                                                 bias=CHAN[:, m, C_BDT:C_BDT + 1]).then_inc(xb_made, 1)
                        act.wait_ge(xb_made, M)
                        nc.scalar.activation(EX[:, :, :], XB[:, :, :], ACT.Abs).then_inc(s_chain, 1)
                        act.wait_ge(s_chain, 1)
                        nc.scalar.activation(EX[:, :, :], EX[:, :, :], ACT.Exp, scale=-1.0).then_inc(ex_made, 1)
                    elif stage == "ln":
                        act.wait_ge(ope_made, 1)
                        nc.scalar.activation(LNO, OPE, ACT.Ln).then_inc(ln_made, 1)
                    elif stage == "decay":
                        if k == 0:
                            act.wait_ge(del_made, 1)
                        for kk in (k, k + 1):
                            if kk >= 2:
                                act.wait_ge(scanned, kk - 1)
                            for m in range(M):
                                ins = nc.scalar.activation(DA[:, kk % 2, m, 1:], DEL[:, m, 1:], ACT.Exp,
                                                           scale=CHAN[:, m, C_A + kk:C_A + kk + 1])
                            ins.then_inc(da_made, 1)
                    elif stage == "square" and k:
                        for tb in range(TB):
                            act.wait_ge(y_added, TB * (E - 1) + tb + 1)
                            nc.scalar.activation(ZN[:, tb, :], Z[:, tb, :], ACT.Square,
                                                 accum_out=SS[:, tb:tb + 1]).then_inc(squares, 1)
                    elif stage == "low":
                        act.wait_ge(zn_turned[k], 1)
                        nc.scalar.activation(ZNT[:, k, 0], ZTP[k][:, :, 0:T], ACT.Copy).then_inc(znt_high[k], 1)
                    elif stage == "weigh":
                        act.wait_ge(lg_shifted[k], 2)
                        nc.scalar.activation(PR[:, :, :], LG[:, :, :], ACT.Exp).then_inc(lg_exped[k], 1)
                    elif stage == "down" and k[0] % E < E - 1:
                        n, half = k
                        for tb in range(2 * half, min(2 * half + 2, TB)):
                            act.wait_ge(y_done, 2 * n + half + 1)
                            if n:
                                act.wait_ge(y_added, TB * (n - 1) + tb + 1)
                            if n == E and tb == 0:
                                act.wait_ge(weighed[1], 1)
                            nc.scalar.activation(YS[:, tb, :], y_out(tb), ACT.Copy,
                                                 scale=COMB[:, n // E, tb, n % E:n % E + 1]).then_inc(y_scaled, 1)
                    elif stage == "up":
                        n, half = k
                        if half == 0:
                            if experts and n >= 2:
                                act.wait_ge(y_done, 2 * (n - 1))
                            if not experts:
                                act.wait_ge(w1_low, KB * E)
                        for fb in (2 * half, 2 * half + 1):
                            act.wait_ge(hidden, FB * (n - ahead) + fb + 1)
                            nc.scalar.activation(HH[:, n % 2, fb, :], HP[:, fb % 2, 0:T], ACT.Silu,
                                                 scale=UNSCALE[:, 0:1]).then_inc(silued, 1)
                    elif stage == "w1_split":
                        act.wait_ge(w1_scaled, 1)
                        act.wait_ge(w1_in[(E + k) % 3], 16 * ((E + k) // 3 + 1))
                        for kb in range(KB):
                            nc.scalar.activation(W1[:, 0, k, kb, :], STAGE[:, (E + k) % 3, kb, :], ACT.Copy,
                                                 scale=WSCALE[:, kb:kb + 1]).then_inc(w1_high, 1)
                    elif stage == "handover":
                        act.wait_ge(z_made, 1)
                        if experts:
                            act.wait_ge(out_made, 1)
                        nc.scalar.activation(H2[:, :, :], H1[:, :, :], ACT.Copy).then_inc(h2_copied, 1)

            run(act, emit, meet)

        @block.vector
        def _(dve):
            v = nc.vector
            dve.wait_ge(weights_in, 16 * 14)
            dve.wait_ge(mask_in, 16)
            v.tensor_tensor(EWT[:, :, :], EWT[:, :, :], MASK, ALU.mult).then_inc(prep_chain, 1)
            v.tensor_copy(PICK[:, :], PICKF[:, :]).then_inc(v_prep, 1)
            v.memset(DA[:, :, :, 0:1], 0.0).then_inc(v_prep, 1)
            v.memset(BC3[0:32, :], 0.0).then_inc(v_prep, 1)
            v.memset(HALF[:, :], -0.5).then_inc(v_prep, 1)
            v.memset(X[F:F + 1, :, :], 1.0).then_inc(v_prep, 1)
            dve.wait_ge(v_prep, 5)
            dve.drain().then_inc(prepared, 1)
            dve.wait_ge(prepared, 3)

            def emit(dve, i, mamba, experts):
                count = [0]

                def link(ins):
                    count[0] += 1
                    ins.then_inc(v_chain, 1)
                    dve.wait_ge(v_chain, count[0])

                def variance(src, var):
                    for tb in range(TB if src is not None else 0):
                        ins = v.bn_stats(STAT[:, tb, :], src[:, tb, :])
                        if tb < TB - 1:
                            ins.then_inc(v_chain, 1)
                            count[0] += 1
                    link(ins)
                    for tb in range(TB):
                        ins = v.bn_aggr(MV[:, tb, :], STAT[:, tb, :])
                        if tb < TB - 1:
                            ins.then_inc(v_chain, 1)
                            count[0] += 1
                    link(ins)
                    v.tensor_scalar(VE[:, :], MV[:, :, 1], LN_EPS, None, ALU.add).then_inc(var, 1)

                def normalise(dst, src, blocks, rstd):
                    dve.wait_ge(rstd, 1)
                    for tb in range(blocks):
                        ins = v.tensor_scalar(dst[:, tb, :], src[:, tb, :], MV[:, tb, 0:1], RSTD[:, tb:tb + 1],
                                              ALU.subtract, ALU.mult)
                        if tb < blocks - 1:
                            ins.then_inc(v_chain, 1)
                            count[0] += 1
                    return ins

                def add_expert(n, half):
                    for tb in range(2 * half, min(2 * half + 2, TB)):
                        dve.wait_ge(y_done, 2 * n + half + 1)
                        dve.wait_ge(y_added, TB * n)
                        v.scalar_tensor_tensor(out=Z[:, tb, :], in0=y_out(tb), scalar=COMB[:, n // E, tb, n % E:n % E + 1],
                                               in1=Z[:, tb, :], op0=ALU.mult, op1=ALU.add).then_inc(y_added, 1)

                def wide(ap):
                    return ap.rearrange("p m t -> p (m t)")

                for stage, k in schedule(mamba, experts):
                    if stage == "project":
                        pj = MP[:, 2 * k:2 * k + 2, :].rearrange("p b (h n) -> p (b h) n", n=D)
                        dve.wait_ge(k_exped, k + 1)
                        dve.wait_ge(q_exped, k + 1)
                        v.tensor_tensor(EK[:, k, 0:D].rearrange("p (h n) -> p h n", h=H),
                                        EK[:, k, D:].rearrange("p (h n) -> p h n", h=H),
                                        pj[:, :, 2 * F:3 * F], ALU.mult).then_inc(kv_made, 1)
                        v.tensor_tensor(RES[:, k, :].rearrange("p (h n) -> p h n", h=H),
                                        ROW[:, 0, :].rearrange("p (h n) -> p h n", h=H),
                                        pj[:, :, 3 * F:4 * F], ALU.add).then_inc(res_made, 1)
                    elif stage == "mix":
                        dve.wait_ge(q_exped, LB)
                        dve.wait_ge(mixed, LB)
                        link(v.scalar_tensor_tensor(out=DD[:, :, :], in0=SG[:, :, :], scalar=1.0,
                                                    in1=MP[:, 0:LB, D:], op0=ALU.add, op1=ALU.mult))
                        link(v.reciprocal(DD[:, :, :], DD[:, :, :]))
                        v.tensor_tensor(YT[:, :, :], DD[:, :, :], MP[:, 0:LB, 0:D], ALU.mult).then_inc(yt_made, 1)
                    elif stage == "mix_out":
                        dve.wait_ge(out_projected, 1)
                        dve.wait_ge(res_made, LB)
                        link(v.tensor_tensor(H1[:, 0:LB, :], RES[:, :, :],
                                             MP[:, 3, :].rearrange("p (b n) -> p b n", b=LB), ALU.add))
                        dve.wait_ge(txt_in, 16)
                        variance(H1, var1)
                        normalise(X2, H1, LB, rstd1).then_inc(h1_scaled, 1)
                        dve.wait_ge(h1_made, 1)
                        variance(H1, var2)
                        normalise(X2, H1, TB, rstd2).then_inc(x2_made, 1)
                    elif stage == "widen_x":
                        dve.wait_ge(widened, k + 1)
                        xin = MP[:, (k + 2) % 4, 0:T]
                        link(v.tensor_scalar(CONV[:, k, :], xin, CHAN[:, k, TAPS - 1:TAPS],
                                             CHAN[:, k, C_CONVB:C_CONVB + 1], ALU.mult, ALU.add))
                        for j in range(1, TAPS):
                            ins = v.scalar_tensor_tensor(out=CONV[:, k, j:], in0=xin[:, 0:T - j],
                                                         scalar=CHAN[:, k, TAPS - 1 - j:TAPS - j],
                                                         in1=CONV[:, k, j:], op0=ALU.mult, op1=ALU.add)
                            if j < TAPS - 1:
                                link(ins)
                            else:
                                ins.then_inc(conv_done, 1)
                    elif stage == "states_in":
                        dve.wait_ge(dt_copied, 1)
                        for q in (1, 2, 3):
                            a, b = 32 * q, 32 * q + 32
                            src = MP[a:b, 2, 0:T]
                            if q == 1:
                                link(v.tensor_copy(BC3[a:b, :], src))
                                continue
                            link(v.tensor_copy(HI[a:b, :], src))
                            if q == 2:
                                link(v.tensor_tensor(BC3[a:b, :], src, HI[a:b, :], ALU.subtract))
                                continue
                            link(v.tensor_tensor(REST[a:b, :], src, HI[a:b, :], ALU.subtract))
                            link(v.tensor_copy(HI[a:b, :], REST[a:b, :]))
                            v.tensor_tensor(BC3[a:b, :], REST[a:b, :], HI[a:b, :], ALU.subtract).then_inc(bc_split, 1)
                    elif stage == "delta":
                        dve.wait_ge(ex_made, 1)
                        v.tensor_scalar(OPE, EX[:, :, :], 1.0, None, ALU.add).then_inc(ope_made, 1)
                        dve.wait_ge(ope_made, 1)
                        link(v.scalar_tensor_tensor(out=wide(EX[:, :, :]), in0=wide(OPE), scalar=-1.0, in1=wide(EX[:, :, :]),
                                                    op0=ALU.add, op1=ALU.subtract))
                        dve.wait_ge(ln_made, 1)
                        link(v.tensor_tensor(EX[:, :, :], LNO, EX[:, :, :], ALU.subtract))
                        v.scalar_tensor_tensor(out=wide(DEL[:, :, :]), in0=wide(XB[:, :, :]), scalar=0.0,
                                               in1=wide(EX[:, :, :]), op0=ALU.max, op1=ALU.add).then_inc(del_made, 1)
                        dve.wait_ge(del_made, 1)
                        dve.wait_ge(u_made, M)
                        link(v.tensor_tensor(DU[:, :, :], DEL[:, :, :], U[:, :, :], ALU.mult))
                    elif stage == "scan_in":
                        dve.wait_ge(bc_cast, k + 1)
                        if k:
                            dve.wait_ge(scanned, k)
                        v.tensor_tensor(DB[:, :, :], DU[:, :, :],
                                        MP[:, k % 2, 0:T].unsqueeze(1).to_broadcast([P, M, T]), ALU.mult)\
                            .then_inc(db_made, 1)
                    elif stage == "scan_run":
                        dve.wait_ge(da_made, k + 1)
                        dve.wait_ge(db_made, k + 1)
                        if k:
                            dve.wait_ge(hc_made, k)
                        v.tensor_tensor_scan(wide(HS[:, :, :]), wide(DA[:, k % 2]), wide(DB[:, :, :]), 0.0,
                                             ALU.mult, ALU.add).then_inc(scanned, 1)
                    elif stage == "scan_out":
                        dve.wait_ge(scanned, k + 1)
                        if k >= 2:
                            dve.wait_ge(y_summed, k - 1)
                        v.tensor_tensor(HC[:, k % 2], HS[:, :, :],
                                        MP[:, 2 + k % 2, 0:T].unsqueeze(1).to_broadcast([P, M, T]), ALU.mult)\
                            .then_inc(hc_made, 1)
                    elif stage == "mamba_out":
                        dve.wait_ge(y_summed, S - 1)
                        dve.wait_ge(hc_made, S)
                        link(v.tensor_tensor(Y[:, :, :], Y[:, :, :], HC[:, (S - 1) % 2], ALU.add))
                        v.tensor_tensor(Y[:, :, :], Y[:, :, :], SZ[:, :, :], ALU.mult).then_inc(y_gated, 1)
                        dve.wait_ge(mamba_projected, 1)
                        link(v.tensor_tensor(X2[:, 0:2, :], X2[:, 0:2, :],
                                             MP[:, 0, :].rearrange("p (b n) -> p b n", b=2), ALU.add))
                        link(v.tensor_tensor(X2[:, 2, :], X2[:, 2, :], MP[:, 1, 0:D], ALU.add))
                        variance(X2, var3)
                        link(normalise(X2, X2, TB, rstd3))
                        link(v.tensor_tensor(X2[:, :, :], X2[:, :, :],
                                             ROW[:, 3:4, :].to_broadcast([P, TB, D]), ALU.mult))
                        link(v.tensor_tensor(X2[:, :, :], X2[:, :, :],
                                             ROW[:, 4:5, :].to_broadcast([P, TB, D]), ALU.add))
                        link(v.tensor_tensor(H1[:, :, :], H1[:, :, :], X2[:, :, :], ALU.add))
                        variance(H1, var4)
                        dve.wait_ge(rstd4, 1)
                        link(v.tensor_tensor(SSE[:, :], MV[:, :, 1], RSTD[:, :], ALU.mult))
                        link(v.tensor_tensor(SSE[:, :], SSE[:, :], RSTD[:, :], ALU.mult))
                        v.tensor_scalar(SSE[:, :], SSE[:, :], RMS_EPS, None, ALU.add).then_inc(ms_made[0], 1)
                        normalise(X2, H1, TB, rstd4).then_inc(z_made, 1)
                        dve.wait_ge(z_made, 1)
                        dve.wait_ge(v_chain, count[0])
                    elif stage == "w1_max":
                        dve.wait_ge(w1_in[k % 3], 16 * (k // 3 + 1))
                        v.tensor_reduce(WMAX[:, k, :], STAGE[:, k % 3], AX, ALU.max, apply_absolute_value=True).then_inc(w1_maxed, 1)
                    elif stage == "w1_scale":
                        link(v.tensor_reduce(WMAX[:, E, :], WRF[:, :, :], AX, ALU.max, apply_absolute_value=True))
                        dve.wait_ge(w1_maxed, E)
                        link(v.tensor_tensor(WMAX[:, :, :], WMAX[:, :, :],
                                             NW[:, :].unsqueeze(1).to_broadcast([P, E + 1, KB]), ALU.mult))
                        v.tensor_reduce(TOPW[:, 0:1], WMAX[:, :, :].rearrange("p e k -> p (e k)"), AX,
                                        ALU.max, apply_absolute_value=True).then_inc(top_in, 1)
                        dve.wait_ge(top_out, 1)
                        link(v.tensor_scalar(TOPW[:, 1:2], TOPW[:, 1:2], 1e-30, None, ALU.max))
                        link(v.tensor_scalar(TOPW[:, 2:3].bitcast(I32), TOPW[:, 1:2].bitcast(I32), 0x7F800000, None,
                                             ALU.bitwise_and))
                        link(v.reciprocal(TOPW[:, 3:4], TOPW[:, 2:3]))
                        link(v.tensor_scalar(UNSCALE[:, :], TOPW[:, 2:3], 1.0 / W_TOP, None, ALU.mult))
                        link(v.tensor_scalar(WSCALE[:, :], NW[:, :], TOPW[:, 3:4], W_TOP, ALU.mult, ALU.mult))
                        v.tensor_tensor(WRF[:, :, :], WRF[:, :, :], WSCALE[:, :].unsqueeze(2).to_broadcast([P, KB, LOG]),
                                        ALU.mult).then_inc(w1_scaled, 1)
                        dve.wait_ge(w1_scaled, 1)
                        link(v.tensor_copy(WR[:, 0], WRF[:, :, :]))
                        link(v.tensor_tensor(WR[:, 1], WRF[:, :, :], WR[:, 0], ALU.subtract))
                    elif stage == "route":
                        if k:
                            dve.wait_ge(squares, TB)
                            v.tensor_scalar(SSE[:, :], SS[:, :], 1.0 / D, RMS_EPS, ALU.mult, ALU.add)\
                                .then_inc(ms_made[1], 1)
                        dve.wait_ge(rms_made[k], 1)
                        for tb in range(TB):
                            v.tensor_scalar(ZN[:, tb, :], (Z if k else X2)[:, tb, :], RMS[:, tb:tb + 1], None,
                                            ALU.mult).then_inc(zn_made[k], 1)
                    elif stage == "low":
                        dve.wait_ge(znt_high[k], 1)
                        v.tensor_tensor(ZNT[:, k, 1], ZTP[k][:, :, 0:T], ZNT[:, k, 0], ALU.subtract)\
                            .then_inc(znt_low[k], 1)
                    elif stage == "weigh":
                        dve.wait_ge(logits_done[k], 1)
                        lgp = LGP[k].rearrange("p (b n) -> p b n", b=TB)
                        link(v.tensor_scalar(LG[:, :, :], lgp, UNSCALE[:, 0:1], None, ALU.mult))
                        link(v.tensor_reduce(MX[:, :, 0], LG[:, :, 0:G], AX, ALU.max))
                        link(v.tensor_reduce(MX[:, :, 1:],
                                             LG[:, :, G:].rearrange("p b (g e) -> p b g e", e=EPG), AX, ALU.max))
                        v.tensor_tensor(LG[:, :, 0:G], LG[:, :, 0:G], MX[:, :, 0:1].to_broadcast([P, TB, G]),
                                        ALU.subtract).then_inc(lg_shifted[k], 1)
                        v.tensor_tensor(LG[:, :, G:].rearrange("p b (g e) -> p b g e", e=EPG),
                                        LG[:, :, G:].rearrange("p b (g e) -> p b g e", e=EPG),
                                        MX[:, :, 1:].unsqueeze(3).to_broadcast([P, TB, G, EPG]),
                                        ALU.subtract).then_inc(lg_shifted[k], 1)
                        dve.wait_ge(lg_exped[k], 1)
                        macro = PR[:, :, 0:G]
                        micro = PR[:, :, G:].rearrange("p b (g e) -> p b g e", e=EPG)
                        link(v.tensor_reduce(SM[:, :, 0], macro, AX, ALU.add))
                        link(v.tensor_reduce(SM[:, :, 1:], micro, AX, ALU.add))
                        link(v.reciprocal(SM[:, :, :], SM[:, :, :]))
                        link(v.tensor_tensor(macro, macro, SM[:, :, 0:1].to_broadcast([P, TB, G]), ALU.mult))
                        link(v.tensor_tensor(micro, micro, SM[:, :, 1:].unsqueeze(3).to_broadcast([P, TB, G, EPG]),
                                             ALU.mult))
                        gt = RK[:, 0].rearrange("p b (g j) -> p b g j", g=G)
                        eq = RK[:, 1].rearrange("p b (g j) -> p b g j", g=G)
                        mine = macro.unsqueeze(3).to_broadcast([P, TB, G, G])
                        other = macro.unsqueeze(2).to_broadcast([P, TB, G, G])
                        link(v.tensor_tensor(gt, other, mine, ALU.is_gt))
                        link(v.tensor_tensor(eq, other, mine, ALU.is_equal))
                        link(v.tensor_tensor(RK[:, 1], RK[:, 1], LOWER[:, :, :], ALU.mult))
                        link(v.tensor_tensor(RK[:, 0], RK[:, 0], RK[:, 1], ALU.add))
                        link(v.tensor_reduce(RANK[:, :, :], gt, AX, ALU.add))
                        kept, lead, share, second, weight = (TOP[:, j] for j in range(5))
                        link(v.scalar_tensor_tensor(out=kept, in0=RANK[:, :, :], scalar=1.5, in1=macro,
                                                    op0=ALU.is_lt, op1=ALU.mult))
                        link(v.tensor_reduce(TS[:, 0], kept, AX, ALU.add))
                        link(v.tensor_scalar(TS[:, 0], TS[:, 0], TOP_EPS, None, ALU.add))
                        link(v.reciprocal(TS[:, 1], TS[:, 0]))
                        link(v.tensor_tensor(kept, kept, TS[:, 1].unsqueeze(2).to_broadcast([P, TB, G]), ALU.mult))
                        link(v.tensor_tensor(lead, micro[:, :, :, 0], micro[:, :, :, 1], ALU.max))
                        link(v.tensor_scalar(share, lead, TOP_EPS, None, ALU.add))
                        link(v.reciprocal(share, share))
                        link(v.tensor_tensor(lead, lead, share, ALU.mult))
                        link(v.tensor_tensor(weight, lead, kept, ALU.mult))
                        link(v.tensor_tensor(second, micro[:, :, :, 1], micro[:, :, :, 0], ALU.is_gt))
                        comb = COMB[:, k].rearrange("p b (g e) -> p b g e", e=EPG)
                        link(v.tensor_tensor(comb[:, :, :, 1], second, weight, ALU.mult))
                        v.tensor_tensor(comb[:, :, :, 0], weight, comb[:, :, :, 1], ALU.subtract).then_inc(weighed[k], 1)
                    elif stage == "w1_split":
                        dve.wait_ge(w1_high, KB * (k + 1))
                        slot = STAGE[:, (E + k) % 3]
                        for kb in range(KB):
                            v.scalar_tensor_tensor(out=W1[:, 1, k, kb, :], in0=slot[:, kb, :], scalar=WSCALE[:, kb:kb + 1],
                                                   in1=W1[:, 0, k, kb, :], op0=ALU.mult, op1=ALU.subtract)\
                                .then_inc(w1_low, 1)
                    elif stage == "down" and k[0] % E == E - 1:
                        add_expert(*k)
                    elif stage == "store":
                        dve.wait_ge(y_added, TB * NX)
                        v.tensor_tensor(OUT[:, :, :], H2[:, :, :], Z[:, :, :], ALU.add).then_inc(out_made, 1)
                    elif stage == "handover":
                        if experts:
                            dve.wait_ge(out_made, 1)
                        link(v.tensor_copy(Z[:, :, :], X2[:, :, :]))

            run(dve, emit, meet)

        @block.gpsimd
        def _(pool):
            pool.wait_ge(prepared, 3)

            def emit(pool, i, mamba, experts):
                g = nc.gpsimd

                def power(dst, src, var, rstd, n):
                    pool.wait_ge(var, n)
                    g.tensor_tensor(dst, src, HALF[:, :], ALU.pow).then_inc(rstd, 1)

                for stage, k in schedule(mamba, experts):
                    if stage == "mix_out":
                        power(RSTD[:, :], VE[:, :], var1, rstd1, 1)
                        pool.wait_ge(h1_scaled, 1)
                        g.tensor_tensor(H1[:, 0:LB, :], X2[:, 0:LB, :], ROW[:, 1:2, :].to_broadcast([P, LB, D]),
                                        ALU.mult).then_inc(g_chain, 1)
                        pool.wait_ge(g_chain, 1)
                        g.tensor_tensor(H1[:, 0:LB, :], H1[:, 0:LB, :], ROW[:, 2:3, :].to_broadcast([P, LB, D]),
                                        ALU.add).then_inc(h1_made, 1)
                        power(RSTD[:, :], VE[:, :], var2, rstd2, 1)
                    elif stage == "states_in":
                        pool.wait_ge(u_made, M)
                        for m in range(M):
                            g.tensor_scalar(Y[:, m, :], U[:, m, :], CHAN[:, m, C_D:C_D + 1], None, ALU.mult)\
                                .then_inc(y_started, 1)
                        pool.wait_ge(y_started, M)
                    elif stage == "sum_y":
                        pool.wait_ge(hc_made, k + 1)
                        if k:
                            pool.wait_ge(y_summed, k)
                        g.tensor_tensor(Y[:, :, :], Y[:, :, :], HC[:, k % 2], ALU.add).then_inc(y_summed, 1)
                    elif stage == "mamba_out":
                        power(RSTD[:, :], VE[:, :], var3, rstd3, 1)
                        power(RSTD[:, :], VE[:, :], var4, rstd4, 1)
                    elif stage == "down" and k[0] % E < E - 1:
                        n, half = k
                        for tb in range(2 * half, min(2 * half + 2, TB)):
                            pool.wait_ge(y_scaled, TB * (n - n // E) + tb + 1)
                            if n:
                                pool.wait_ge(y_added, TB * (n - 1) + tb + 1)
                            g.tensor_tensor(Z[:, tb, :], Z[:, tb, :], YS[:, tb, :], ALU.add).then_inc(y_added, 1)
                    elif stage == "route":
                        power(RMS[:, :], SSE[:, :], ms_made[k], rms_made[k], 1)
                    elif stage == "w1_scale":
                        pool.wait_ge(top_in, 1)
                        g.partition_all_reduce(TOPW[:, 1:2], TOPW[:, 0:1], P, bass.bass_isa.ReduceOp.max)\
                            .then_inc(top_out, 1)

            def meet_pool(pool, i):
                pool.wait_ge(arrived, 4)
                pool.drain()
                pool.sem_clear(range(first, last + 1))
                pool.sem_clear(arrived)
                pool.sem_inc(go, 1)

            run(pool, emit, meet_pool)


def _blocks(a, p=P):
    import numpy as np
    return np.ascontiguousarray(np.moveaxis(a.reshape(-1, p, *a.shape[1:]), 0, 1))


def kernel(**inputs):
    import numpy as np
    import concourse.bacc as bacc
    from concourse.bass_utils import run_bass_kernel_spmd as run

    a = {k: np.asarray(v) for k, v in inputs.items()}
    t = {k.replace("L0_", ""): v for k, v in a.items()}
    eye = np.eye(F, dtype=np.float32)
    w_qkv = np.zeros((F + 1, 4 * F), np.float32)
    for j, n in enumerate("qkv"):
        w_qkv[:F, j * F:(j + 1) * F] = t[f"tok_W{n}_w"].T
        w_qkv[F, j * F:(j + 1) * F] = t[f"tok_W{n}_b"]
    w_qkv[:F, 3 * F:] = eye
    rows = np.stack([t["tok_out_b"], t["tok_ln_g"], t["tok_ln_b"], t["attn_gamma"], t["attn_beta"]])
    chan = np.concatenate([t["attn_conv_w"], t["attn_conv_b"][:, None], t["attn_b_dt"][:, None],
                           t["attn_D"][:, None], t["attn_A_log"]], axis=1)
    wx = t["attn_W_x"]
    w_x = np.zeros((DIN, P), np.float32)
    w_x[:, :R] = wx[:, :R]
    for q in (1, 2, 3):
        w_x[:, 32 * q:32 * q + 32] = wx[:, R:]
    w_route = np.concatenate([t["ffn_w_macro"], t["ffn_w_micro"].reshape(E, D)], axis=0).T
    pick = np.zeros((P, 2 * S), np.float32)
    for q in (1, 2, 3):
        pick[32 * q + np.arange(32), np.arange(32)] = 1.0
    lower = np.tril(np.ones((G, G), np.float32), -1).reshape(1, 1, G * G)
    mask_words = np.zeros((P, LB, L, 4), np.uint8)
    mask_words[..., 0] = _blocks(t["tok_local_mask"].T)
    arrays = {
        "x": np.concatenate([a["x"], a["x"][:1]]).transpose(0, 1, 3, 2),
        "txt": a["txt"],
        "w_qkv": w_qkv,
        "w_bias_t": _blocks(t["tok_w_bias"].T),
        "mask_t": mask_words.view(np.int32)[..., 0],
        "out_w": _blocks(t["tok_out_w"]),
        "rows": np.broadcast_to(rows, (P, *rows.shape)),
        "w_in": _blocks(t["attn_W_in"]),
        "chan": _blocks(chan),
        "w_x": _blocks(w_x),
        "w_dt": t["attn_W_dt"],
        "w_out": _blocks(t["attn_W_out"]),
        "w_route": _blocks(np.ascontiguousarray(w_route)),
        "norm_w": _blocks(t["ffn_norm_w"]),
        "w1": t["ffn_w1"].reshape(E, FF, KB, P).transpose(3, 0, 2, 1),
        "w2": t["ffn_w2"].reshape(E, D, FB, P).transpose(3, 0, 2, 1),
        "ident": np.eye(P, dtype=np.float32),
        "pick": pick,
        "lower": np.broadcast_to(lower, (P, TB, G * G)),
    }
    arrays = {k: np.ascontiguousarray(v) for k, v in arrays.items()}
    nc = bacc.Bacc("TRN2", target_bir_lowering=False, num_devices=1)
    args = [nc.dram_tensor(f"in_{k}", v.shape, mybir.dt.from_np(v.dtype), kind="ExternalInput").ap()
            for k, v in arrays.items()]
    args.append(nc.dram_tensor("out_h", (B, T, D), F32, kind="ExternalOutput").ap())
    fusion_kernel(nc, *args)
    r = run(nc, [{f"in_{k}": v for k, v in arrays.items()}], core_ids=[0])
    return r.results[0]["out_h"]
```

```python
from contextlib import ExitStack

import concourse.bass as bass
from concourse import mybir

F32 = mybir.dt.float32
BF16 = mybir.dt.bfloat16
F16 = mybir.dt.float16
I32 = mybir.dt.int32
ACT = mybir.ActivationFunctionType
ALU = mybir.AluOpType
AX = mybir.AxisListType.X

P = 128
B, F, L, H = 8, 64, 256, 4
LT = 128
D = H * F
T = L + LT
TB = T // P
LB = L // P
KB = D // P
DIN = 2 * D
M = DIN // P
S = 16
R = D // 16
TAPS = 4
G, EPG = 4, 2
E = G * EPG
FF = 512
FB = FF // P
LOOPS = 2
NX = LOOPS * E
LOG = G + E
W_TOP = 2.0 ** 14
LN_EPS, RMS_EPS, TOP_EPS = 1e-5, 1e-6, 1e-9

ROWS = ("out_b", "ln_g", "ln_b", "gamma", "beta")
C_CONV, C_CONVB, C_BDT, C_D, C_A = 0, TAPS, TAPS + 1, TAPS + 2, TAPS + 3
CH = TAPS + 3 + S

BESIDE = [
    (0, "project", 0), (0, "project", 1), (1, "mix", 0), (3, "turn_mixed", 0), (4, "mix_out", 0),
    (9, "turn_x2", 0), (10, "widen_x", 0), (10, "widen_x", 1), (10, "widen_x", 2), (10, "widen_x", 3),
    (10, "u", 0), (10, "u", 1), (11, "u", 2), (12, "u", 3), (13, "states_in", 0), (14, "delta", 0),
    (15, "ln", 0), (15, "widen_z", 0),
]
for pair, (at, then) in enumerate(((17, 19), (21, 23), (25, 27), (28, 32), (35, 37), (39, 41), (43, 46), (49, 51))):
    BESIDE += [(at, "decay", 2 * pair), (at, "scan", 2 * pair), (then, "scan", 2 * pair + 1)]
BESIDE += [(55, "mamba_out", 0), (56, "power3", 0), (58, "power4", 0), (59, "power_z", 0), (60, "route", 0), (60, "low", 0)]
BETWEEN = 6


def schedule(mamba, experts):
    beside = [(at, name, k) for at, name, k in BESIDE if mamba]
    steps = [("load", 0)] if mamba else []

    def piece(name):
        return [(name, BETWEEN)] if mamba else []

    if not experts:
        order = [(name, k) for _, name, k in beside]
        for before, maxima in (("mix", 2), ("mix_out", 3), ("widen_x", 3)):
            for _ in range(maxima):
                order.insert(order.index((before, 0)), ("w1_max", sum(name == "w1_max" for name, _ in order)))
        order.insert(order.index(("widen_x", 0)), ("w1_scale", 0))
        at = order.index(("widen_z", 0)) + 1
        order[at:at] = [("widen_z", m) for m in range(1, M)]
        for e in range(E):
            order.insert(order.index(("decay", 2 * e)) + 1, ("w1_split", e))
        steps += order
    else:
        steps += [("logits", 0), ("shift", 0)] + [beside.pop(0)[1:] for _ in range(2 * mamba)]
        units = [("weigh", 0)]
        for n in range(1, NX + 1):
            ups = [("up", n, 0), ("up", n, 1)] if n < NX else []
            downs = [("down", n - 1, 0), ("down", n - 1, 1)]
            if n == E:
                gate = [("widen_z", m) for m in range(1, M)] if mamba else []
                units += downs + piece("scan_in") + [("square", 1)] + gate[:2] + [("route", 1)] + piece("scan_run")
                units += [("low", 1)] + gate[2:] + piece("scan_out") + ups[:1] + [("logits", 1), ("shift", 1)] + ups[1:]
                units += [("weigh", 1)]
            elif n == 3:
                units += ups + downs
            else:
                for j in range(2):
                    units += ups[j:j + 1] + downs[j:j + 1]
        units.append(("store", 0))
        done = 0
        for unit in units:
            while unit[0] in ("up", "down") and beside and beside[0][0] <= done:
                steps.append(beside.pop(0)[1:])
            steps.append(unit)
            done += unit[0] in ("up", "down")
        steps += [one[1:] for one in beside]
    steps = [one if len(one) == 2 else (one[0], one[1:]) for one in steps]
    if mamba:
        steps += [("up", (NX, 0)), ("up", (NX, 1)), ("handover", 0)]
    placed = []
    for name, k in steps:
        placed.append((name, k))
        if name == "scan":
            if k != BETWEEN or not experts:
                placed += [("scan_in", k), ("scan_run", k), ("scan_out", k)]
            if k:
                placed.append(("sum_y", k - 1))
    return placed


def fusion_kernel(nc, x, txt, w_qkv, w_bias_t, mask_t, out_w, rows, w_in, chan, w_x, w_dt, w_out,
                  w_route, norm_w, w1, w2, ident, pick, lower, out):
    with ExitStack() as ctx:
        def sb(name, shape, dt=F32):
            return ctx.enter_context(nc.sbuf_tensor(name, shape, dt))

        def pb(name, shape):
            return ctx.enter_context(nc.psum_tensor(name, shape, F32))

        sems = {}

        def sem(name):
            sems[name] = ctx.enter_context(nc.semaphore(name))
            return sems[name]

        W1 = sb("W1", [P, 2, E, KB, FF], F16)
        W2 = sb("W2", [P, E, FB, D])
        WIN = sb("WIN", [P, KB, 2 * DIN])
        WX = sb("WX", [P, M, P])
        WDT = sb("WDT", [R, DIN])
        WOUT = sb("WOUT", [P, M, D])
        OW = sb("OW", [P, KB, D])
        WQ = sb("WQ", [F + 1, 4 * F])
        EWT = sb("EWT", [P, LB, L])
        ROW = sb("ROW", [P, len(ROWS), D])
        CHAN = sb("CHAN", [P, M, CH])
        WRF = sb("WRF", [P, KB, LOG])
        WR = sb("WR", [P, 2, KB, LOG], F16)
        NW = sb("NW", [P, KB])
        WMAX = sb("WMAX", [P, E + 1, KB])
        TOPW = sb("TOPW", [P, 4])
        WSCALE = sb("WSCALE", [P, KB])
        UNSCALE = sb("UNSCALE", [P, 1])
        IDENT = sb("IDENT", [P, P])
        PICKF = sb("PICKF", [P, 2 * S])
        PICK = sb("PICK", [P, 2 * S], BF16)
        LOWER = sb("LOWER", [P, TB, G * G])
        HALF = sb("HALF", [P, TB])
        X = sb("X", [F + 1, H, L])
        YTT = sb("YTT", [P, KB, L])
        H1 = sb("H1", [P, TB, D])
        X2 = sb("X2", [P, TB, D])
        X2T = sb("X2T", [P, KB, T])
        STAT = sb("STAT", [P, TB, 6])
        MV = sb("MV", [P, TB, 2])
        VE = sb("VE", [P, TB])
        RSTD = sb("RSTD", [P, TB])
        U = sb("U", [P, M, T])
        SZ = sb("SZ", [P, M, T])
        DT = sb("DT", [R, T])
        BC3 = sb("BC3", [P, T], BF16)
        DEL = sb("DEL", [P, M, T])
        DU = sb("DU", [P, M, T])
        Y = sb("Y", [P, M, T])
        DA = sb("DA", [P, 2, M, T])
        DB = sb("DB", [P, M, T])
        HS = sb("HS", [P, M, T])
        HC = sb("HC", [P, 2, M, T])
        XB, EX, CONV = DB, HS, HS
        OPE, LNO = HC[:, 0], HC[:, 1]
        scratch = HC[:, :, :, :].rearrange("p a m t -> p (a m t)")
        EK = scratch[:, 0:1024].rearrange("p (b n) -> p b n", b=LB)
        SG = scratch[:, 1024:1536].rearrange("p (b n) -> p b n", b=LB)
        RES = scratch[:, 1536:2048].rearrange("p (b n) -> p b n", b=LB)
        YT = scratch[:, 2048:2560].rearrange("p (b n) -> p b n", b=LB)
        DD = scratch[:, 2560:3072].rearrange("p (b n) -> p b n", b=LB)
        REST = scratch[:, 2048:2048 + T]
        HI = scratch[:, 2560:2560 + T // 2].bitcast(BF16)
        MASK = scratch[:, 0:LB * L].bitcast(I32).rearrange("p (b n) -> p b n", b=LB)
        H2 = sb("H2", [P, TB, D])
        Z = sb("Z", [P, TB, D])
        ZN = sb("ZN", [P, TB, D])
        OUT = scratch[:, 0:TB * D].rearrange("p (b n) -> p b n", b=TB)
        ZNT = sb("ZNT", [P, LOOPS, 2, KB, T], F16)
        HH = sb("HH", [P, 2, FB, T])
        STAGE = HH[:, :, :, :].rearrange("p a f t -> p (a f t)").rearrange("p (s k n) -> p s k n", s=3, k=KB)
        SS = sb("SS", [P, TB])
        SSE = sb("SSE", [P, TB])
        RMS = sb("RMS", [P, TB])
        LG = sb("LG", [P, TB, LOG])
        PR = sb("PR", [P, TB, LOG])
        MX = sb("MX", [P, TB, 1 + G])
        SM = sb("SM", [P, TB, 1 + G])
        RK = sb("RK", [P, 2, TB, G * G])
        RANK = sb("RANK", [P, TB, G])
        TOP = sb("TOP", [P, 5, TB, G])
        TS = sb("TS", [P, 2, TB])
        YS = sb("YS", [P, TB, D])
        COMB = sb("COMB", [P, LOOPS, TB, E])

        HP = pb("HP", [P, 2, 512])
        YP = pb("YP", [P, 2, 512])
        MP = pb("MP", [P, 4, 512])

        def y_out(tb):
            return YP[:, tb // 2, (tb % 2) * D:(tb % 2 + 1) * D]

        BANKS = (3, 0, 1, 3)
        GATE_BANK = (MP[:, 1, 0:T], HP[:, 0, 0:T], HP[:, 1, 0:T], YP[:, 0, 0:T])
        ZTP = (MP[:, 2:4], HP)
        LGP = YP[:, 1, D:D + TB * LOG]

        weights_in = ctx.enter_context(nc.semaphore("weights_in"))
        early_in = ctx.enter_context(nc.semaphore("early_in"))
        prepared_late = ctx.enter_context(nc.semaphore("prepared_late"))
        w2_in = ctx.enter_context(nc.semaphore("w2_in"))
        v_prep = ctx.enter_context(nc.semaphore("v_prep"))
        prepared = ctx.enter_context(nc.semaphore("prepared"))
        prep_chain = ctx.enter_context(nc.semaphore("prep_chain"))
        arrived = ctx.enter_context(nc.semaphore("arrived"))
        go = ctx.enter_context(nc.semaphore("go"))
        sp_seen = ctx.enter_context(nc.semaphore("sp_seen"))

        x_in = sem("x_in")
        txt_in = sem("txt_in")
        v_chain = sem("v_chain")
        g_chain = sem("g_chain")
        proj_done = sem("proj_done")
        q_exped = sem("q_exped")
        k_exped = sem("k_exped")
        kv_made = sem("kv_made")
        res_made = sem("res_made")
        mixed = sem("mixed")
        yt_made = sem("yt_made")
        yt_turned = sem("yt_turned")
        ytt_copied = sem("ytt_copied")
        out_projected = sem("out_projected")
        var1, rstd1 = sem("var1"), sem("rstd1")
        var2, rstd2 = sem("var2"), sem("rstd2")
        var3, rstd3 = sem("var3"), sem("rstd3")
        var4, rstd4 = sem("var4"), sem("rstd4")
        h1_scaled = sem("h1_scaled")
        h1_made = sem("h1_made")
        x2_made = sem("x2_made")
        x2_turned = sem("x2_turned")
        x2t_copied = sem("x2t_copied")
        widened = sem("widened")
        z_widened = sem("z_widened")
        tap_made = sem("tap_made")
        conv_done = sem("conv_done")
        u_made = sem("u_made")
        sz_made = sem("sz_made")
        dbc_done = sem("dbc_done")
        dt_copied = sem("dt_copied")
        bc_split = sem("bc_split")
        delta_done = sem("delta_done")
        abs_made = sem("abs_made")
        xb_made = sem("xb_made")
        ex_made = sem("ex_made")
        ope_made = sem("ope_made")
        ln_made = sem("ln_made")
        del_made = sem("del_made")
        y_started = sem("y_started")
        bc_cast = sem("bc_cast")
        da_made = sem("da_made")
        db_made = sem("db_made")
        scanned = sem("scanned")
        hc_made = sem("hc_made")
        y_summed = sem("y_summed")
        y_gated = sem("y_gated")
        mamba_projected = sem("mamba_projected")
        h2_copied = sem("h2_copied")
        ms_made = [sem(f"ms_made{j}") for j in range(LOOPS)]
        rms_made = [sem(f"rms_made{j}") for j in range(LOOPS)]
        zn_made = [sem(f"zn_made{j}") for j in range(LOOPS)]
        zn_turned = [sem(f"zn_turned{j}") for j in range(LOOPS)]
        znt_high = [sem(f"znt_high{j}") for j in range(LOOPS)]
        znt_low = [sem(f"znt_low{j}") for j in range(LOOPS)]
        logits_done = [sem(f"logits_done{j}") for j in range(LOOPS)]
        lg_shifted = [sem(f"lg_shifted{j}") for j in range(LOOPS)]
        lg_exped = [sem(f"lg_exped{j}") for j in range(LOOPS)]
        weighed = [sem(f"weighed{j}") for j in range(LOOPS)]
        squares = sem("squares")
        z_made = sem("z_made")
        w1_in = [sem(f"w1_in{j}") for j in range(3)]
        w1_maxed = sem("w1_maxed")
        top_in, top_out = sem("top_in"), sem("top_out")
        w1_scaled = sem("w1_scaled")
        w1_timed = sem("w1_timed")
        w1_high, w1_low = sem("w1_high"), sem("w1_low")
        hidden = sem("hidden")
        silued = sem("silued")
        y_done = sem("y_done")
        y_scaled = sem("y_scaled")
        y_added = sem("y_added")
        out_made = sem("out_made")
        stored = sem("stored")
        first, last = min(s.num for s in sems.values()), max(s.num for s in sems.values())
        assert last - first + 1 == len(sems)

        def run(eng, emit, meet):
            emit(eng, 0, True, False)
            meet(eng, 0)
            with eng.Fori(1, B) as i:
                emit(eng, i, True, True)
                meet(eng, i)
            emit(eng, B, False, True)

        def meet(eng, i):
            eng.drain().then_inc(arrived, 1)
            eng.wait_ge(go, i + 1)

        EARLY = [(EWT[:, :, :], w_bias_t), (X[0:F, :, :], x[0]), (WQ[:, :], w_qkv), (ROW[:, :, :], rows)]
        LATER = [(IDENT[:, :], ident), (OW[:, :, :], out_w), (WIN[:, :, :], w_in), (CHAN[:, :, :], chan),
                 (WX[:, :, :], w_x), (WDT[:, :], w_dt), (PICKF[:, :], pick), (WRF[:, :, :], w_route),
                 (NW[:, :], norm_w), (WOUT[:, :, :], w_out), (LOWER[:, :, :], lower)]

        def weights_ready(eng):
            eng.wait_ge(weights_in, 16 * len(LATER))

        block = ctx.enter_context(nc.Block())

        @block.sync
        def _(sp):
            sp.dma_start(MASK, mask_t).then_inc(early_in, 16)
            for dst, src in EARLY:
                sp.dma_start(dst, src).then_inc(early_in, 16)
            for dst, src in LATER:
                sp.dma_start(dst, src).then_inc(weights_in, 16)

            def emit(eng, i, mamba, experts):
                for stage, _k in schedule(mamba, experts):
                    if stage == "load":
                        ti = txt[i] if isinstance(i, int) else txt[bass.ds(i, 1), :, :].rearrange("a t d -> (a t) d")
                        eng.dma_start(H1[:, LB, :], ti).then_inc(txt_in, 16)
                    if stage == "turn_mixed":
                        eng.wait_ge(proj_done, LB)
                        xi = x[i + 1] if isinstance(i, int) else \
                            x[bass.ds(i + 1, 1), :, :, :].rearrange("a c h l -> (a c) h l")
                        eng.dma_start(X[0:F, :, :], xi).then_inc(x_in, 16)
                    if stage in ("w1_max", "w1_split"):
                        n = _k + (E if stage == "w1_split" else 0)
                        if 3 <= n < E + 3:
                            eng.wait_ge(w1_maxed, n - 2)
                        if n >= E + 3:
                            eng.wait_ge(w1_low, n - E - 2)
                        eng.dma_start(STAGE[:, n % 3], w1[:, _k]).then_inc(w1_in[n % 3], 16)
                    if stage == "mamba_out" and not experts:
                        eng.dma_start(W2[:, :, :, :], w2).then_inc(w2_in, 16)
                        eng.wait_ge(w2_in, 16)
                    if stage == "handover":
                        eng.wait_ge(x_in, 16)
                    if stage == "store":
                        eng.wait_ge(out_made, 1)
                        if isinstance(i, int):
                            oi = out[i - 1].rearrange("(b p) d -> p b d", p=P)
                        else:
                            oi = out[bass.ds(i - 1, 1), :, :].rearrange("a (b p) d -> p (a b) d", p=P)
                        eng.dma_start(oi, OUT[:, :, :]).then_inc(stored, 16)
                        eng.wait_ge(stored, 16)

            def meet_sp(eng, i):
                turn = i + 1 if isinstance(i, int) else eng.snap(i + 1)
                eng.sem_inc(arrived, 1)
                eng.wait_ge(go, turn)
                eng.sem_inc(sp_seen, 1)

            run(sp, emit, meet_sp)

        @block.tensor
        def _(pe):
            pe.wait_ge(prepared, 2)

            def stay_warm(bank, n):
                for _ in range(n):
                    nc.tensor.matmul(bank, W1[:, 0, 0, 0, 0:P], ZNT[:, 0, 0, 0, :], start=True, stop=True)

            pe.wait_ge(early_in, 16 * (len(EARLY) + 1))

            def emit(pe, i, mamba, experts):
                ahead = 1 if experts else NX

                def mix_matmul(out_, lhsT, rhs, k, n):
                    return nc.tensor.matmul(out_, lhsT, rhs, start=(k == 0), stop=(k == n - 1))

                def second_layer(n, half):
                    if n:
                        pe.wait_ge(silued, FB * (n + 1 - ahead))
                    if n % E:
                        pe.wait_ge(y_scaled, TB * (n - 1 - n // E) + min(2 * half + 2, TB))
                    if n == E:
                        pe.wait_ge(y_added, TB * n)
                        if mamba:
                            pe.wait_ge(sz_made, M)
                    if n % E == 0 and half:
                        pe.wait_ge(lg_shifted[n // E], 2)
                    for tb in range(2 * half, min(2 * half + 2, TB)):
                        for fb in range(FB):
                            mm = mix_matmul(y_out(tb), HH[:, n % 2, fb, tb * P:(tb + 1) * P], W2[:, n % E, fb, :], fb, FB)
                    mm.then_inc(y_done, 1)

                for stage, k in schedule(mamba, experts):
                    if stage == "project":
                        for h in range(H):
                            mm = mix_matmul(MP[:, 2 * k + h // 2, (h % 2) * D:(h % 2 + 1) * D],
                                            X[:, h, k * P:(k + 1) * P], WQ[:, :], 0, 1)
                        mm.then_inc(proj_done, 1)
                    elif stage == "mix":
                        pe.wait_ge(kv_made, LB)
                        pe.wait_ge(res_made, LB)
                        pe.wait_ge(q_exped, LB)
                        for tb in range(LB):
                            for s in range(LB):
                                mm = mix_matmul(MP[:, tb, :], EWT[:, s, tb * P:(tb + 1) * P], EK[:, s, :], s, LB)
                            mm.then_inc(mixed, 1)
                    elif stage == "turn_mixed":
                        if not experts:
                            weights_ready(pe)
                        pe.wait_ge(yt_made, 1)
                        for kb in range(KB):
                            for tb in range(LB):
                                mm = nc.tensor.transpose(MP[:, 2, kb * L + tb * P:kb * L + (tb + 1) * P],
                                                         YT[:, tb, kb * P:(kb + 1) * P], IDENT[:, :])
                        mm.then_inc(yt_turned, 1)
                    elif stage == "mix_out":
                        pe.wait_ge(ytt_copied, 1)
                        for tb in range(LB):
                            for kb in range(KB):
                                mm = mix_matmul(MP[:, 3, tb * D:(tb + 1) * D], YTT[:, kb, tb * P:(tb + 1) * P],
                                                OW[:, kb, :], kb, KB)
                        mm.then_inc(out_projected, 1)
                    elif stage == "turn_x2":
                        pe.wait_ge(x2_made, 1)
                        for kb in range(KB):
                            for tb in range(TB):
                                mm = nc.tensor.transpose(MP[:, kb, tb * P:(tb + 1) * P],
                                                         X2[:, tb, kb * P:(kb + 1) * P], IDENT[:, :])
                        mm.then_inc(x2_turned, 1)
                    elif stage == "widen_x":
                        pe.wait_ge(x2t_copied, 1)
                        for kb in range(KB):
                            mm = mix_matmul(MP[:, (k + 2) % 4, 0:T], WIN[:, kb, k * P:(k + 1) * P], X2T[:, kb, :], kb, KB)
                        mm.then_inc(widened, 1)
                    elif stage == "states_in":
                        pe.wait_ge(u_made, M)
                        for m in range(M):
                            mm = mix_matmul(MP[:, 2, 0:T], WX[:, m, :], U[:, m, :], m, M)
                        mm.then_inc(dbc_done, 1)
                    elif stage == "delta":
                        pe.wait_ge(dt_copied, 1)
                        for m in range(M):
                            if m == M - 1:
                                pe.wait_ge(xb_made, 1)
                            mix_matmul(MP[:, BANKS[m], 0:T], WDT[:, m * P:(m + 1) * P], DT[:, :], 0, 1)\
                                .then_inc(delta_done, 1)
                    elif stage == "widen_z":
                        if k == 0:
                            pe.wait_ge(xb_made, 3)
                        elif experts and k < 3:
                            pe.wait_ge(silued, FB * (E - ahead))
                        elif experts:
                            pe.wait_ge(y_added, TB * E)
                        for kb in range(KB):
                            mm = mix_matmul(GATE_BANK[k], WIN[:, kb, (M + k) * P:(M + k + 1) * P], X2T[:, kb, :], kb, KB)
                        mm.then_inc(z_widened, 1)
                    elif stage == "scan":
                        if k == 0:
                            pe.wait_ge(xb_made, M)
                            pe.wait_ge(bc_split, 1)
                            if not experts:
                                pe.wait_ge(prepared_late, 2)
                        if k == 1:
                            pe.wait_ge(sz_made, 1)
                        if k >= 2:
                            pe.wait_ge(db_made, k - 1)
                        mix_matmul(MP[:, k % 2, 0:T], PICK[:, k:k + 1].to_broadcast([P, P]), BC3[:, :], 0, 1)
                        if k >= 2:
                            pe.wait_ge(hc_made, k - 1)
                        mix_matmul(MP[:, 2 + k % 2, 0:T], PICK[:, S + k:S + k + 1].to_broadcast([P, P]), BC3[:, :], 0, 1)\
                            .then_inc(bc_cast, 1)
                    elif stage == "mamba_out":
                        pe.wait_ge(y_gated, 1)
                        for tb in range(TB):
                            for m in range(M):
                                mm = mix_matmul(MP[:, tb // 2, (tb % 2) * D:(tb % 2 + 1) * D],
                                                Y[:, m, tb * P:(tb + 1) * P], WOUT[:, m, :], m, M)
                            if tb:
                                mm.then_inc(mamba_projected, 1)
                    elif stage == "route":
                        if k:
                            pe.wait_ge(silued, FB * (E - ahead))
                            if mamba:
                                pe.wait_ge(sz_made, 3)
                            else:
                                stay_warm(HP[:, 0, 0:T], 20)
                        for tb in range(TB):
                            pe.wait_ge(zn_made[k], tb + 1)
                            for kb in range(KB):
                                mm = nc.tensor.transpose(ZTP[k][:, kb, tb * P:(tb + 1) * P],
                                                         ZN[:, tb, kb * P:(kb + 1) * P], IDENT[:, :])
                        mm.then_inc(zn_turned[k], 1)
                        if k and not mamba:
                            pe.wait_ge(y_added, TB * E)
                            stay_warm(YP[:, 0, 0:T], 12)
                    elif stage == "logits":
                        if k:
                            pe.wait_ge(y_added, TB * E)
                            pe.wait_ge(znt_low[k], 1)
                        for tb in range(TB):
                            for kb in range(KB):
                                for j, (a, b) in enumerate(((0, 0), (0, 1), (1, 0))):
                                    mm = mix_matmul(LGP[:, tb * LOG:(tb + 1) * LOG],
                                                    ZNT[:, k, a, kb, tb * P:(tb + 1) * P],
                                                    WR[:, b, kb, :], 3 * kb + j, 3 * KB)
                        mm.then_inc(logits_done[k], 1)
                    elif stage == "up":
                        n, half = k
                        if half == 0 and n % E == 0:
                            pe.wait_ge(znt_low[n // E % LOOPS], 1)
                        for fb in (2 * half, 2 * half + 1):
                            before = FB * (n - ahead) + fb - 2
                            if before >= 0 and (n % E or half):
                                pe.wait_ge(silued, before + 1)
                            for kb in range(KB):
                                for j, (a, b) in enumerate(((0, 0), (0, 1), (1, 0))):
                                    mm = mix_matmul(HP[:, fb % 2, 0:T], W1[:, a, n % E, kb, fb * P:(fb + 1) * P],
                                                    ZNT[:, n // E % LOOPS, b, kb, :], 3 * kb + j, 3 * KB)
                            mm.then_inc(hidden, 1)
                    elif stage == "down":
                        second_layer(*k)

            def meet_pe(pe, i):
                pe.drain().then_inc(arrived, 1)
                stay_warm(MP[:, 3, 0:T], 13)
                pe.wait_ge(go, i + 1)

            run(pe, emit, meet_pe)

        @block.scalar
        def _(act):
            act.wait_ge(prep_chain, 1)
            nc.scalar.activation(EWT[:, :, :], EWT[:, :, :], ACT.Exp).then_inc(prepared, 1)
            act.wait_ge(prepared, 2)

            def prepare_late():
                act.wait_ge(weights_in, 16 * len(LATER))
                nc.scalar.activation(CHAN[:, :, C_A:], CHAN[:, :, C_A:], ACT.Exp).then_inc(prep_chain, 1)
                act.wait_ge(prep_chain, 2)
                nc.scalar.mul(CHAN[:, :, C_A:], CHAN[:, :, C_A:], -1.0).then_inc(prepared_late, 1)
                weights_ready(act)

            def emit(act, i, mamba, experts):
                ahead = 1 if experts else NX
                for stage, k in schedule(mamba, experts):
                    if stage == "project":
                        act.wait_ge(proj_done, k + 1)
                        pj = MP[:, 2 * k:2 * k + 2, :].rearrange("p b (h n) -> p (b h) n", n=D)
                        nc.scalar.activation(EK[:, k, D:].rearrange("p (h n) -> p h n", h=H), pj[:, :, F:2 * F],
                                             ACT.Exp).then_inc(k_exped, 1)
                        nc.scalar.activation(SG[:, k, :].rearrange("p (h n) -> p h n", h=H), pj[:, :, 0:F],
                                             ACT.Exp, scale=-1.0).then_inc(q_exped, 1)
                    elif stage == "turn_mixed":
                        if not experts:
                            prepare_late()
                        act.wait_ge(yt_turned, 1)
                        nc.scalar.activation(YTT[:, :, :].rearrange("p k t -> p (k t)"), MP[:, 2, :],
                                             ACT.Copy).then_inc(ytt_copied, 1)
                    elif stage == "turn_x2":
                        act.wait_ge(x2_turned, 1)
                        nc.scalar.activation(X2T[:, :, :], MP[:, 0:KB, 0:T], ACT.Copy).then_inc(x2t_copied, 1)
                    elif stage == "widen_x":
                        act.wait_ge(widened, k + 1)
                        nc.scalar.activation(CONV[:, k, :], MP[:, (k + 2) % 4, 0:T], ACT.Identity,
                                             bias=CHAN[:, k, C_CONVB:C_CONVB + 1],
                                             scale=CHAN[:, k, TAPS - 1:TAPS]).then_inc(tap_made, 1)
                    elif stage == "u":
                        act.wait_ge(conv_done, k + 1)
                        nc.scalar.activation(U[:, k, :], CONV[:, k, :], ACT.Silu).then_inc(u_made, 1)
                    elif stage == "widen_z":
                        act.wait_ge(z_widened, k + 1)
                        nc.scalar.activation(SZ[:, k, :], GATE_BANK[k], ACT.Silu).then_inc(sz_made, 1)
                    elif stage == "states_in":
                        act.wait_ge(dbc_done, 1)
                        nc.scalar.activation(DT[:, :], MP[0:R, 2, 0:T], ACT.Copy).then_inc(dt_copied, 1)
                    elif stage == "delta":
                        for m in range(M):
                            act.wait_ge(delta_done, m + 1)
                            if m == 0:
                                act.wait_ge(u_made, M)
                            nc.scalar.activation(EX[:, m, :], MP[:, BANKS[m], 0:T], ACT.Abs,
                                                 bias=CHAN[:, m, C_BDT:C_BDT + 1]).then_inc(abs_made, 1)
                        act.wait_ge(abs_made, M)
                        nc.scalar.activation(EX[:, :, :], EX[:, :, :], ACT.Exp, scale=-1.0).then_inc(ex_made, 1)
                    elif stage == "ln":
                        act.wait_ge(ope_made, 1)
                        nc.scalar.activation(LNO, OPE, ACT.Ln).then_inc(ln_made, 1)
                    elif stage == "decay":
                        if k == 0:
                            act.wait_ge(del_made, 1)
                            if not experts:
                                act.wait_ge(prepared_late, 2)
                        for kk in (k, k + 1):
                            if kk >= 2:
                                act.wait_ge(scanned, kk - 1)
                            for m in range(M):
                                ins = nc.scalar.activation(DA[:, kk % 2, m, 1:], DEL[:, m, 1:], ACT.Exp,
                                                           scale=CHAN[:, m, C_A + kk:C_A + kk + 1])
                            ins.then_inc(da_made, 1)
                    elif stage == "square" and k:
                        for tb in range(TB):
                            act.wait_ge(y_added, TB * (E - 1) + tb + 1)
                            nc.scalar.activation(ZN[:, tb, :], Z[:, tb, :], ACT.Square,
                                                 accum_out=SS[:, tb:tb + 1]).then_inc(squares, 1)
                    elif stage == "low":
                        act.wait_ge(zn_turned[k], 1)
                        nc.scalar.activation(ZNT[:, k, 0], ZTP[k][:, :, 0:T], ACT.Copy).then_inc(znt_high[k], 1)
                    elif stage == "shift":
                        act.wait_ge(lg_shifted[k], 2)
                        nc.scalar.activation(PR[:, :, :], LG[:, :, :], ACT.Exp).then_inc(lg_exped[k], 1)
                    elif stage == "down" and k[0] % E < E - 1:
                        n, half = k
                        for tb in range(2 * half, min(2 * half + 2, TB)):
                            act.wait_ge(y_done, 2 * n + half + 1)
                            if n:
                                act.wait_ge(y_added, TB * (n - 1) + tb + 1)
                            if n % E == 0 and tb == 0:
                                act.wait_ge(weighed[n // E], 1)
                            nc.scalar.activation(YS[:, tb, :], y_out(tb), ACT.Copy,
                                                 scale=COMB[:, n // E, tb, n % E:n % E + 1]).then_inc(y_scaled, 1)
                    elif stage == "up":
                        n, half = k
                        if half == 0:
                            if experts and n >= 2:
                                act.wait_ge(y_done, 2 * (n - 1))
                            if not experts:
                                act.wait_ge(w1_low, E)
                        for fb in (2 * half, 2 * half + 1):
                            act.wait_ge(hidden, FB * (n - ahead) + fb + 1)
                            nc.scalar.activation(HH[:, n % 2, fb, :], HP[:, fb % 2, 0:T], ACT.Silu,
                                                 scale=UNSCALE[:, 0:1]).then_inc(silued, 1)
                    elif stage == "w1_split":
                        act.wait_ge(w1_scaled, 1)
                        act.wait_ge(w1_in[(E + k) % 3], 16 * ((E + k) // 3 + 1))
                        slot = STAGE[:, (E + k) % 3]
                        for kb in range(KB):
                            nc.scalar.activation(slot[:, kb, :], slot[:, kb, :], ACT.Copy,
                                                 scale=WSCALE[:, kb:kb + 1]).then_inc(w1_timed, 1)
                        act.wait_ge(w1_timed, KB * (k + 1))
                        nc.scalar.activation(W1[:, 0, k], slot, ACT.Copy).then_inc(w1_high, 1)
                    elif stage == "handover":
                        act.wait_ge(z_made, 1)
                        if experts:
                            act.wait_ge(out_made, 1)
                        nc.scalar.activation(H2[:, :, :], H1[:, :, :], ACT.Copy).then_inc(h2_copied, 1)

            run(act, emit, meet)

        @block.vector
        def _(dve):
            v = nc.vector
            dve.wait_ge(early_in, 16 * (len(EARLY) + 1))
            v.tensor_tensor(EWT[:, :, :], EWT[:, :, :], MASK, ALU.mult).then_inc(prep_chain, 1)
            v.memset(DA[:, :, :, 0:1], 0.0).then_inc(v_prep, 1)
            v.memset(BC3[0:32, :], 0.0).then_inc(v_prep, 1)
            v.memset(HALF[:, :], -0.5).then_inc(v_prep, 1)
            v.memset(X[F:F + 1, :, :], 1.0).then_inc(v_prep, 1)
            dve.wait_ge(v_prep, 4)
            dve.drain().then_inc(prepared, 1)
            dve.wait_ge(prepared, 2)

            def emit(dve, i, mamba, experts):
                count = [0]

                def link(ins):
                    count[0] += 1
                    ins.then_inc(v_chain, 1)
                    dve.wait_ge(v_chain, count[0])

                def variance(src, var):
                    for tb in range(TB if src is not None else 0):
                        ins = v.bn_stats(STAT[:, tb, :], src[:, tb, :])
                        if tb < TB - 1:
                            ins.then_inc(v_chain, 1)
                            count[0] += 1
                    link(ins)
                    for tb in range(TB):
                        ins = v.bn_aggr(MV[:, tb, :], STAT[:, tb, :])
                        if tb < TB - 1:
                            ins.then_inc(v_chain, 1)
                            count[0] += 1
                    link(ins)
                    v.tensor_scalar(VE[:, :], MV[:, :, 1], LN_EPS, None, ALU.add).then_inc(var, 1)

                def normalise(dst, src, blocks, rstd):
                    dve.wait_ge(rstd, 1)
                    for tb in range(blocks):
                        ins = v.tensor_scalar(dst[:, tb, :], src[:, tb, :], MV[:, tb, 0:1], RSTD[:, tb:tb + 1],
                                              ALU.subtract, ALU.mult)
                        if tb < blocks - 1:
                            ins.then_inc(v_chain, 1)
                            count[0] += 1
                    return ins

                def add_expert(n, half):
                    for tb in range(2 * half, min(2 * half + 2, TB)):
                        dve.wait_ge(y_done, 2 * n + half + 1)
                        dve.wait_ge(y_added, TB * n)
                        v.scalar_tensor_tensor(out=Z[:, tb, :], in0=y_out(tb), scalar=COMB[:, n // E, tb, n % E:n % E + 1],
                                               in1=Z[:, tb, :], op0=ALU.mult, op1=ALU.add).then_inc(y_added, 1)

                def wide(ap):
                    return ap.rearrange("p m t -> p (m t)")

                for stage, k in schedule(mamba, experts):
                    if stage == "project":
                        pj = MP[:, 2 * k:2 * k + 2, :].rearrange("p b (h n) -> p (b h) n", n=D)
                        dve.wait_ge(k_exped, k + 1)
                        dve.wait_ge(q_exped, k + 1)
                        v.tensor_tensor(EK[:, k, 0:D].rearrange("p (h n) -> p h n", h=H),
                                        EK[:, k, D:].rearrange("p (h n) -> p h n", h=H),
                                        pj[:, :, 2 * F:3 * F], ALU.mult).then_inc(kv_made, 1)
                        v.tensor_tensor(RES[:, k, :].rearrange("p (h n) -> p h n", h=H),
                                        ROW[:, 0, :].rearrange("p (h n) -> p h n", h=H),
                                        pj[:, :, 3 * F:4 * F], ALU.add).then_inc(res_made, 1)
                    elif stage == "mix":
                        dve.wait_ge(q_exped, LB)
                        dve.wait_ge(mixed, LB)
                        link(v.scalar_tensor_tensor(out=DD[:, :, :], in0=SG[:, :, :], scalar=1.0,
                                                    in1=MP[:, 0:LB, D:], op0=ALU.add, op1=ALU.mult))
                        link(v.reciprocal(DD[:, :, :], DD[:, :, :]))
                        v.tensor_tensor(YT[:, :, :], DD[:, :, :], MP[:, 0:LB, 0:D], ALU.mult).then_inc(yt_made, 1)
                    elif stage == "turn_mixed" and not experts:
                        dve.wait_ge(weights_in, 16 * len(LATER))
                        v.tensor_copy(PICK[:, :], PICKF[:, :]).then_inc(prepared_late, 1)
                        weights_ready(dve)
                    elif stage == "mix_out":
                        dve.wait_ge(out_projected, 1)
                        dve.wait_ge(res_made, LB)
                        link(v.tensor_tensor(H1[:, 0:LB, :], RES[:, :, :],
                                             MP[:, 3, :].rearrange("p (b n) -> p b n", b=LB), ALU.add))
                        dve.wait_ge(txt_in, 16)
                        variance(H1, var1)
                        normalise(X2, H1, LB, rstd1).then_inc(h1_scaled, 1)
                        dve.wait_ge(h1_made, 1)
                        variance(H1, var2)
                        normalise(X2, H1, TB, rstd2).then_inc(x2_made, 1)
                    elif stage == "widen_x":
                        dve.wait_ge(tap_made, k + 1)
                        xin = MP[:, (k + 2) % 4, 0:T]
                        for j in range(1, TAPS):
                            ins = v.scalar_tensor_tensor(out=CONV[:, k, j:], in0=xin[:, 0:T - j],
                                                         scalar=CHAN[:, k, TAPS - 1 - j:TAPS - j],
                                                         in1=CONV[:, k, j:], op0=ALU.mult, op1=ALU.add)
                            if j < TAPS - 1:
                                link(ins)
                            else:
                                ins.then_inc(conv_done, 1)
                    elif stage == "states_in":
                        dve.wait_ge(dt_copied, 1)
                        for q in (1, 2, 3):
                            a, b = 32 * q, 32 * q + 32
                            src = MP[a:b, 2, 0:T]
                            if q == 1:
                                link(v.tensor_copy(BC3[a:b, :], src))
                                continue
                            link(v.tensor_copy(HI[a:b, :], src))
                            if q == 2:
                                link(v.tensor_tensor(BC3[a:b, :], src, HI[a:b, :], ALU.subtract))
                                continue
                            link(v.tensor_tensor(REST[a:b, :], src, HI[a:b, :], ALU.subtract))
                            link(v.tensor_copy(HI[a:b, :], REST[a:b, :]))
                            v.tensor_tensor(BC3[a:b, :], REST[a:b, :], HI[a:b, :], ALU.subtract).then_inc(bc_split, 1)
                    elif stage == "delta":
                        for m in range(M):
                            dve.wait_ge(abs_made, m + 1)
                            v.tensor_scalar(XB[:, m, :], MP[:, BANKS[m], 0:T], CHAN[:, m, C_BDT:C_BDT + 1], None,
                                            ALU.add).then_inc(xb_made, 1)
                        dve.wait_ge(xb_made, M)
                        dve.wait_ge(ex_made, 1)
                        v.tensor_scalar(OPE, EX[:, :, :], 1.0, None, ALU.add).then_inc(ope_made, 1)
                        dve.wait_ge(ope_made, 1)
                        link(v.scalar_tensor_tensor(out=wide(EX[:, :, :]), in0=wide(OPE), scalar=-1.0, in1=wide(EX[:, :, :]),
                                                    op0=ALU.add, op1=ALU.subtract))
                        link(v.scalar_tensor_tensor(out=wide(EX[:, :, :]), in0=wide(XB[:, :, :]), scalar=0.0,
                                                    in1=wide(EX[:, :, :]), op0=ALU.max, op1=ALU.subtract))
                        dve.wait_ge(ln_made, 1)
                        v.tensor_tensor(DEL[:, :, :], LNO, EX[:, :, :], ALU.add).then_inc(del_made, 1)
                        dve.wait_ge(del_made, 1)
                        dve.wait_ge(u_made, M)
                        link(v.tensor_tensor(DU[:, :, :], DEL[:, :, :], U[:, :, :], ALU.mult))
                    elif stage == "scan_in":
                        dve.wait_ge(bc_cast, k + 1)
                        if k:
                            dve.wait_ge(scanned, k)
                        v.tensor_tensor(DB[:, :, :], DU[:, :, :],
                                        MP[:, k % 2, 0:T].unsqueeze(1).to_broadcast([P, M, T]), ALU.mult)\
                            .then_inc(db_made, 1)
                    elif stage == "scan_run":
                        dve.wait_ge(da_made, k + 1)
                        dve.wait_ge(db_made, k + 1)
                        if k:
                            dve.wait_ge(hc_made, k)
                        v.tensor_tensor_scan(wide(HS[:, :, :]), wide(DA[:, k % 2]), wide(DB[:, :, :]), 0.0,
                                             ALU.mult, ALU.add).then_inc(scanned, 1)
                    elif stage == "scan_out":
                        dve.wait_ge(scanned, k + 1)
                        if k >= 2:
                            dve.wait_ge(y_summed, k - 1)
                        v.tensor_tensor(HC[:, k % 2], HS[:, :, :],
                                        MP[:, 2 + k % 2, 0:T].unsqueeze(1).to_broadcast([P, M, T]), ALU.mult)\
                            .then_inc(hc_made, 1)
                    elif stage == "mamba_out":
                        dve.wait_ge(y_summed, S - 1)
                        dve.wait_ge(hc_made, S)
                        dve.wait_ge(sz_made, M)
                        link(v.tensor_tensor(Y[:, :, :], Y[:, :, :], HC[:, (S - 1) % 2], ALU.add))
                        v.tensor_tensor(Y[:, :, :], Y[:, :, :], SZ[:, :, :], ALU.mult).then_inc(y_gated, 1)
                        link(v.tensor_tensor(H1[:, :, :], H1[:, :, :],
                                             ROW[:, 4:5, :].to_broadcast([P, TB, D]), ALU.add))
                        dve.wait_ge(mamba_projected, 1)
                        link(v.tensor_tensor(X2[:, 0:2, :], X2[:, 0:2, :],
                                             MP[:, 0, :].rearrange("p (b n) -> p b n", b=2), ALU.add))
                        dve.wait_ge(mamba_projected, 2)
                        link(v.tensor_tensor(X2[:, 2, :], X2[:, 2, :], MP[:, 1, 0:D], ALU.add))
                        variance(X2, var3)
                        link(normalise(X2, X2, TB, rstd3))
                        link(v.tensor_tensor(X2[:, :, :], X2[:, :, :],
                                             ROW[:, 3:4, :].to_broadcast([P, TB, D]), ALU.mult))
                        link(v.tensor_tensor(H1[:, :, :], H1[:, :, :], X2[:, :, :], ALU.add))
                        variance(H1, var4)
                        dve.wait_ge(rstd4, 1)
                        link(v.tensor_tensor(SSE[:, :], MV[:, :, 1], RSTD[:, :], ALU.mult))
                        link(v.tensor_tensor(SSE[:, :], SSE[:, :], RSTD[:, :], ALU.mult))
                        v.tensor_scalar(SSE[:, :], SSE[:, :], RMS_EPS, None, ALU.add).then_inc(ms_made[0], 1)
                        normalise(X2, H1, TB, rstd4).then_inc(z_made, 1)
                        dve.wait_ge(z_made, 1)
                        dve.wait_ge(v_chain, count[0])
                    elif stage == "w1_max":
                        dve.wait_ge(w1_in[k % 3], 16 * (k // 3 + 1))
                        v.tensor_reduce(WMAX[:, k, :], STAGE[:, k % 3], AX, ALU.max, apply_absolute_value=True).then_inc(w1_maxed, 1)
                    elif stage == "w1_scale":
                        link(v.tensor_reduce(WMAX[:, E, :], WRF[:, :, :], AX, ALU.max, apply_absolute_value=True))
                        dve.wait_ge(w1_maxed, E)
                        link(v.tensor_tensor(WMAX[:, :, :], WMAX[:, :, :],
                                             NW[:, :].unsqueeze(1).to_broadcast([P, E + 1, KB]), ALU.mult))
                        v.tensor_reduce(TOPW[:, 0:1], WMAX[:, :, :].rearrange("p e k -> p (e k)"), AX,
                                        ALU.max, apply_absolute_value=True).then_inc(top_in, 1)
                        dve.wait_ge(top_out, 1)
                        link(v.tensor_scalar(TOPW[:, 1:2], TOPW[:, 1:2], 1e-30, None, ALU.max))
                        link(v.tensor_scalar(TOPW[:, 2:3].bitcast(I32), TOPW[:, 1:2].bitcast(I32), 0x7F800000, None,
                                             ALU.bitwise_and))
                        link(v.reciprocal(TOPW[:, 3:4], TOPW[:, 2:3]))
                        link(v.tensor_scalar(UNSCALE[:, :], TOPW[:, 2:3], 1.0 / W_TOP, None, ALU.mult))
                        link(v.tensor_scalar(WSCALE[:, :], NW[:, :], TOPW[:, 3:4], W_TOP, ALU.mult, ALU.mult))
                        v.tensor_tensor(WRF[:, :, :], WRF[:, :, :], WSCALE[:, :].unsqueeze(2).to_broadcast([P, KB, LOG]),
                                        ALU.mult).then_inc(w1_scaled, 1)
                        dve.wait_ge(w1_scaled, 1)
                        link(v.tensor_copy(WR[:, 0], WRF[:, :, :]))
                        link(v.tensor_tensor(WR[:, 1], WRF[:, :, :], WR[:, 0], ALU.subtract))
                    elif stage == "route":
                        if k:
                            dve.wait_ge(squares, TB)
                            v.tensor_scalar(SSE[:, :], SS[:, :], 1.0 / D, RMS_EPS, ALU.mult, ALU.add)\
                                .then_inc(ms_made[1], 1)
                        dve.wait_ge(rms_made[k], 1)
                        for tb in range(TB):
                            v.tensor_scalar(ZN[:, tb, :], (Z if k else X2)[:, tb, :], RMS[:, tb:tb + 1], None,
                                            ALU.mult).then_inc(zn_made[k], 1)
                    elif stage == "low":
                        dve.wait_ge(znt_high[k], 1)
                        v.tensor_tensor(ZNT[:, k, 1], ZTP[k][:, :, 0:T], ZNT[:, k, 0], ALU.subtract)\
                            .then_inc(znt_low[k], 1)
                    elif stage == "shift":
                        dve.wait_ge(logits_done[k], 1)
                        lgp = LGP.rearrange("p (b n) -> p b n", b=TB)
                        link(v.tensor_scalar(LG[:, :, :], lgp, UNSCALE[:, 0:1], None, ALU.mult))
                        link(v.tensor_reduce(MX[:, :, 0], LG[:, :, 0:G], AX, ALU.max))
                        link(v.tensor_reduce(MX[:, :, 1:],
                                             LG[:, :, G:].rearrange("p b (g e) -> p b g e", e=EPG), AX, ALU.max))
                        v.tensor_tensor(LG[:, :, 0:G], LG[:, :, 0:G], MX[:, :, 0:1].to_broadcast([P, TB, G]),
                                        ALU.subtract).then_inc(lg_shifted[k], 1)
                        v.tensor_tensor(LG[:, :, G:].rearrange("p b (g e) -> p b g e", e=EPG),
                                        LG[:, :, G:].rearrange("p b (g e) -> p b g e", e=EPG),
                                        MX[:, :, 1:].unsqueeze(3).to_broadcast([P, TB, G, EPG]),
                                        ALU.subtract).then_inc(lg_shifted[k], 1)
                    elif stage == "weigh":
                        dve.wait_ge(lg_exped[k], 1)
                        macro = PR[:, :, 0:G]
                        micro = PR[:, :, G:].rearrange("p b (g e) -> p b g e", e=EPG)
                        link(v.tensor_reduce(SM[:, :, 0], macro, AX, ALU.add))
                        link(v.tensor_reduce(SM[:, :, 1:], micro, AX, ALU.add))
                        link(v.reciprocal(SM[:, :, :], SM[:, :, :]))
                        link(v.tensor_tensor(macro, macro, SM[:, :, 0:1].to_broadcast([P, TB, G]), ALU.mult))
                        link(v.tensor_tensor(micro, micro, SM[:, :, 1:].unsqueeze(3).to_broadcast([P, TB, G, EPG]),
                                             ALU.mult))
                        gt = RK[:, 0].rearrange("p b (g j) -> p b g j", g=G)
                        eq = RK[:, 1].rearrange("p b (g j) -> p b g j", g=G)
                        mine = macro.unsqueeze(3).to_broadcast([P, TB, G, G])
                        other = macro.unsqueeze(2).to_broadcast([P, TB, G, G])
                        link(v.tensor_tensor(gt, other, mine, ALU.is_gt))
                        link(v.tensor_tensor(eq, other, mine, ALU.is_equal))
                        link(v.tensor_tensor(RK[:, 1], RK[:, 1], LOWER[:, :, :], ALU.mult))
                        link(v.tensor_tensor(RK[:, 0], RK[:, 0], RK[:, 1], ALU.add))
                        link(v.tensor_reduce(RANK[:, :, :], gt, AX, ALU.add))
                        kept, lead, share, second, weight = (TOP[:, j] for j in range(5))
                        link(v.scalar_tensor_tensor(out=kept, in0=RANK[:, :, :], scalar=1.5, in1=macro,
                                                    op0=ALU.is_lt, op1=ALU.mult))
                        link(v.tensor_reduce(TS[:, 0], kept, AX, ALU.add))
                        link(v.tensor_scalar(TS[:, 0], TS[:, 0], TOP_EPS, None, ALU.add))
                        link(v.reciprocal(TS[:, 1], TS[:, 0]))
                        link(v.tensor_tensor(kept, kept, TS[:, 1].unsqueeze(2).to_broadcast([P, TB, G]), ALU.mult))
                        link(v.tensor_tensor(lead, micro[:, :, :, 0], micro[:, :, :, 1], ALU.max))
                        link(v.tensor_scalar(share, lead, TOP_EPS, None, ALU.add))
                        link(v.reciprocal(share, share))
                        link(v.tensor_tensor(lead, lead, share, ALU.mult))
                        link(v.tensor_tensor(weight, lead, kept, ALU.mult))
                        link(v.tensor_tensor(second, micro[:, :, :, 1], micro[:, :, :, 0], ALU.is_gt))
                        comb = COMB[:, k].rearrange("p b (g e) -> p b g e", e=EPG)
                        link(v.tensor_tensor(comb[:, :, :, 1], second, weight, ALU.mult))
                        v.tensor_tensor(comb[:, :, :, 0], weight, comb[:, :, :, 1], ALU.subtract).then_inc(weighed[k], 1)
                    elif stage == "down" and k[0] % E == E - 1:
                        add_expert(*k)
                    elif stage == "store":
                        dve.wait_ge(y_added, TB * NX)
                        v.tensor_tensor(OUT[:, :, :], H2[:, :, :], Z[:, :, :], ALU.add).then_inc(out_made, 1)
                    elif stage == "handover":
                        if experts:
                            dve.wait_ge(out_made, 1)
                        link(v.tensor_copy(Z[:, :, :], X2[:, :, :]))

            run(dve, emit, meet)

        @block.gpsimd
        def _(pool):
            pool.wait_ge(prepared, 2)
            pool.wait_ge(early_in, 16 * (len(EARLY) + 1))

            def emit(pool, i, mamba, experts):
                g = nc.gpsimd

                def power(dst, src, var, rstd, n):
                    pool.wait_ge(var, n)
                    g.tensor_tensor(dst, src, HALF[:, :], ALU.pow).then_inc(rstd, 1)

                for stage, k in schedule(mamba, experts):
                    if stage == "turn_mixed" and not experts:
                        weights_ready(pool)
                    elif stage == "mix_out":
                        power(RSTD[:, :], VE[:, :], var1, rstd1, 1)
                        pool.wait_ge(h1_scaled, 1)
                        g.tensor_tensor(H1[:, 0:LB, :], X2[:, 0:LB, :], ROW[:, 1:2, :].to_broadcast([P, LB, D]),
                                        ALU.mult).then_inc(g_chain, 1)
                        pool.wait_ge(g_chain, 1)
                        g.tensor_tensor(H1[:, 0:LB, :], H1[:, 0:LB, :], ROW[:, 2:3, :].to_broadcast([P, LB, D]),
                                        ALU.add).then_inc(h1_made, 1)
                        power(RSTD[:, :], VE[:, :], var2, rstd2, 1)
                    elif stage == "states_in":
                        pool.wait_ge(u_made, M)
                        for m in range(M):
                            g.tensor_scalar(Y[:, m, :], U[:, m, :], CHAN[:, m, C_D:C_D + 1], None, ALU.mult)\
                                .then_inc(y_started, 1)
                        pool.wait_ge(y_started, M)
                    elif stage == "sum_y":
                        pool.wait_ge(hc_made, k + 1)
                        if k:
                            pool.wait_ge(y_summed, k)
                        g.tensor_tensor(Y[:, :, :], Y[:, :, :], HC[:, k % 2], ALU.add).then_inc(y_summed, 1)
                    elif stage == "power3":
                        power(RSTD[:, :], VE[:, :], var3, rstd3, 1)
                    elif stage == "power4":
                        power(RSTD[:, :], VE[:, :], var4, rstd4, 1)
                    elif stage == "down" and k[0] % E < E - 1:
                        n, half = k
                        for tb in range(2 * half, min(2 * half + 2, TB)):
                            pool.wait_ge(y_scaled, TB * (n - n // E) + tb + 1)
                            if n:
                                pool.wait_ge(y_added, TB * (n - 1) + tb + 1)
                            g.tensor_tensor(Z[:, tb, :], Z[:, tb, :], YS[:, tb, :], ALU.add).then_inc(y_added, 1)
                    elif stage == "power_z" or (stage == "route" and k):
                        power(RMS[:, :], SSE[:, :], ms_made[k], rms_made[k], 1)
                    elif stage == "w1_scale":
                        pool.wait_ge(top_in, 1)
                        g.partition_all_reduce(TOPW[:, 1:2], TOPW[:, 0:1], P, bass.bass_isa.ReduceOp.max)\
                            .then_inc(top_out, 1)
                    elif stage == "w1_split":
                        pool.wait_ge(w1_high, k + 1)
                        g.tensor_tensor(W1[:, 1, k], STAGE[:, (E + k) % 3], W1[:, 0, k], ALU.subtract).then_inc(w1_low, 1)

            def meet_pool(pool, i):
                pool.wait_ge(arrived, 4)
                pool.drain()
                pool.sem_clear(range(first, last + 1))
                pool.sem_clear(arrived)
                pool.sem_inc(go, 1)

            run(pool, emit, meet_pool)


def _blocks(a, p=P):
    import numpy as np
    return np.ascontiguousarray(np.moveaxis(a.reshape(-1, p, *a.shape[1:]), 0, 1))


def kernel(**inputs):
    import numpy as np
    import concourse.bacc as bacc
    from concourse.bass_utils import run_bass_kernel_spmd as run

    a = {k: np.asarray(v) for k, v in inputs.items()}
    t = {k.replace("L0_", ""): v for k, v in a.items()}
    eye = np.eye(F, dtype=np.float32)
    w_qkv = np.zeros((F + 1, 4 * F), np.float32)
    for j, n in enumerate("qkv"):
        w_qkv[:F, j * F:(j + 1) * F] = t[f"tok_W{n}_w"].T
        w_qkv[F, j * F:(j + 1) * F] = t[f"tok_W{n}_b"]
    w_qkv[:F, 3 * F:] = eye
    rows = np.stack([t["tok_out_b"], t["tok_ln_g"], t["tok_ln_b"], t["attn_gamma"], t["attn_beta"]])
    chan = np.concatenate([t["attn_conv_w"], t["attn_conv_b"][:, None], t["attn_b_dt"][:, None],
                           t["attn_D"][:, None], t["attn_A_log"]], axis=1)
    wx = t["attn_W_x"]
    w_x = np.zeros((DIN, P), np.float32)
    w_x[:, :R] = wx[:, :R]
    for q in (1, 2, 3):
        w_x[:, 32 * q:32 * q + 32] = wx[:, R:]
    w_route = np.concatenate([t["ffn_w_macro"], t["ffn_w_micro"].reshape(E, D)], axis=0).T
    pick = np.zeros((P, 2 * S), np.float32)
    for q in (1, 2, 3):
        pick[32 * q + np.arange(32), np.arange(32)] = 1.0
    lower = np.tril(np.ones((G, G), np.float32), -1).reshape(1, 1, G * G)
    mask_words = np.zeros((P, LB, L, 4), np.uint8)
    mask_words[..., 0] = _blocks(t["tok_local_mask"].T)
    arrays = {
        "x": np.concatenate([a["x"], a["x"][:1]]).transpose(0, 1, 3, 2),
        "txt": a["txt"],
        "w_qkv": w_qkv,
        "w_bias_t": _blocks(t["tok_w_bias"].T),
        "mask_t": mask_words.view(np.int32)[..., 0],
        "out_w": _blocks(t["tok_out_w"]),
        "rows": np.broadcast_to(rows, (P, *rows.shape)),
        "w_in": _blocks(t["attn_W_in"]),
        "chan": _blocks(chan),
        "w_x": _blocks(w_x),
        "w_dt": t["attn_W_dt"],
        "w_out": _blocks(t["attn_W_out"]),
        "w_route": _blocks(np.ascontiguousarray(w_route)),
        "norm_w": _blocks(t["ffn_norm_w"]),
        "w1": t["ffn_w1"].reshape(E, FF, KB, P).transpose(3, 0, 2, 1),
        "w2": t["ffn_w2"].reshape(E, D, FB, P).transpose(3, 0, 2, 1),
        "ident": np.eye(P, dtype=np.float32),
        "pick": pick,
        "lower": np.broadcast_to(lower, (P, TB, G * G)),
    }
    arrays = {k: np.ascontiguousarray(v) for k, v in arrays.items()}
    nc = bacc.Bacc("TRN2", target_bir_lowering=False, num_devices=1)
    args = [nc.dram_tensor(f"in_{k}", v.shape, mybir.dt.from_np(v.dtype), kind="ExternalInput").ap()
            for k, v in arrays.items()]
    args.append(nc.dram_tensor("out_h", (B, T, D), F32, kind="ExternalOutput").ap())
    fusion_kernel(nc, *args)
    r = run(nc, [{f"in_{k}": v for k, v in arrays.items()}], core_ids=[0])
    return r.results[0]["out_h"]
```
